# Optimizing a Trainium2 kernel written in Bass

```python
import numpy as np
import jax
import jax.numpy as jnp

def _softmax(x, axis=-1):
    return jax.nn.softmax(x, axis=axis)

def _gelu(x):
    return jax.nn.gelu(x, approximate=True)

def _silu(x):
    return jax.nn.silu(x)

def _sigmoid(x):
    return jax.nn.sigmoid(x)

def _layernorm(x, axis=-1, eps=1e-05):
    m = jnp.mean(x, axis=axis, keepdims=True)
    v = jnp.var(x, axis=axis, keepdims=True)
    return (x - m) / jnp.sqrt(v + eps)

def _scatter_add(tgt, idx, src, axis=0):
    return tgt.at[idx].add(src)

def _segment_sum(src, seg, n):
    return jax.ops.segment_sum(src, seg, n)
kernel_name = 'mk_seq_preln_d1_jaxref_r8_5134b7'

def setup_inputs(seed: int=0):
    np.random.seed(seed)
    _w = jnp.asarray

    def _L0_attn_setup():
        import jax, jax.numpy as jnp
        from jax import lax
        import numpy as np
        B, T, C = (8, 256, 128)
        ATT_SCALE = 1.0
        LN_EPS = 1e-05

        def _layernorm(x, g, b):
            mu = jnp.mean(x, axis=-1, keepdims=True)
            var = jnp.mean(jnp.square(x - mu), axis=-1, keepdims=True)
            return (x - mu) * lax.rsqrt(var + LN_EPS) * g + b

        def _wkv_scan(k, v, td):
            kT = jnp.swapaxes(k, 0, 1)
            vT = jnp.swapaxes(v, 0, 1)

            def step(carry, kv):
                num, den = carry
                kt, vt = kv
                den = den * td + kt
                num = num * td + kt * vt
                return ((num, den), num / (den + 1e-08))
            z = jnp.zeros((k.shape[0], k.shape[2]), dtype=k.dtype)
            _, wkvT = lax.scan(step, (z, z), (kT, vT))
            return jnp.swapaxes(wkvT, 0, 1)

        def _reference_tuple_inner(x, time_decay, time_mix_k, time_mix_v, time_mix_r, Wk, Wv, Wr, Wo, ln_g, ln_b):
            x = _layernorm(x, ln_g, ln_b)
            last_x = jnp.pad(x[:, :-1], ((0, 0), (1, 0), (0, 0)))
            k = (x * time_mix_k + last_x * (1.0 - time_mix_k)) @ Wk.T
            v = (x * time_mix_v + last_x * (1.0 - time_mix_v)) @ Wv.T
            r = (x * time_mix_r + last_x * (1.0 - time_mix_r)) @ Wr.T
            k = k * ATT_SCALE
            td = jnp.exp(time_decay)
            wkv = _wkv_scan(jnp.exp(k), v, td)
            out = jax.nn.sigmoid(r) * wkv @ Wo.T
            new_state = x[:, -1:]
            return (out, new_state)
        key = jax.random.key(seed)
        ks = jax.random.split(key, 10)
        scale = 1.0 / np.sqrt(C)
        x = jax.random.normal(ks[0], (B, T, C), dtype=jnp.float32)
        Wk = jax.random.normal(ks[1], (C, C), dtype=jnp.float32) * scale
        Wv = jax.random.normal(ks[2], (C, C), dtype=jnp.float32) * scale
        Wr = jax.random.normal(ks[3], (C, C), dtype=jnp.float32) * scale
        Wo = jax.random.normal(ks[4], (C, C), dtype=jnp.float32) * scale
        decay_init = jnp.linspace(0.1, 0.45, C, dtype=jnp.float32)
        time_decay = jnp.log(decay_init / (1.0 - decay_init))
        time_mix_k = jax.random.uniform(ks[5], (1, 1, C), dtype=jnp.float32) * 0.375
        time_mix_v = jax.random.uniform(ks[6], (1, 1, C), dtype=jnp.float32) * 0.5
        time_mix_r = jax.random.uniform(ks[7], (1, 1, C), dtype=jnp.float32) * 0.375
        ln_g = jnp.ones((C,), dtype=jnp.float32)
        ln_b = jnp.zeros((C,), dtype=jnp.float32)
        return {'x': x, 'time_decay': time_decay, 'time_mix_k': time_mix_k, 'time_mix_v': time_mix_v, 'time_mix_r': time_mix_r, 'Wk': Wk, 'Wv': Wv, 'Wr': Wr, 'Wo': Wo, 'ln_g': ln_g, 'ln_b': ln_b}
    _L0_attn_in = _L0_attn_setup()

    def _L0_ffn_setup():
        import jax, jax.numpy as jnp
        import numpy as np
        NUM_NOD = 6
        MAX_PREV = 5
        NUM_EDGE = 20
        D = 128
        H = 8
        LN_EPS = 1e-06

        def _layernorm(x, g, b):
            mu = jnp.mean(x, axis=-1, keepdims=True)
            var = jnp.mean(jnp.square(x - mu), axis=-1, keepdims=True)
            return (x - mu) * jax.lax.rsqrt(var + LN_EPS) * g + b

        def _mha(q, k, v, wq, wk, wv, wo):
            B, S, d = q.shape
            dh = d // H
            qh = (q @ wq).reshape(B, S, H, dh)
            kh = (k @ wk).reshape(B, S, H, dh)
            vh = (v @ wv).reshape(B, S, H, dh)
            scores = jnp.einsum('bqhd,bkhd->bhqk', qh, kh) / jnp.sqrt(jnp.asarray(dh, q.dtype))
            attn = jax.nn.softmax(scores, axis=-1)
            ctx = jnp.einsum('bhqk,bkhd->bqhd', attn, vh).reshape(B, S, d)
            return ctx @ wo
        key = jax.random.key(seed)
        ks = jax.random.split(key, 12)
        B, S = (8, 128)
        scale = 1.0 / np.sqrt(D)
        return {'inputs': jax.random.normal(ks[0], (B, S, D), jnp.float32), 'ew': jax.random.uniform(ks[1], (NUM_NOD, 3), jnp.float32), 'act_w': jax.random.uniform(ks[2], (NUM_NOD,), jnp.float32), 'We': jax.random.normal(ks[3], (NUM_EDGE, D, D), jnp.float32) * scale, 'be': jnp.zeros((NUM_EDGE, D), jnp.float32), 'Wq': jax.random.normal(ks[4], (NUM_NOD, D, D), jnp.float32) * scale, 'Wk': jax.random.normal(ks[5], (NUM_NOD, D, D), jnp.float32) * scale, 'Wv': jax.random.normal(ks[6], (NUM_NOD, D, D), jnp.float32) * scale, 'Wo': jax.random.normal(ks[7], (NUM_NOD, D, D), jnp.float32) * scale, 'ln_g': jnp.ones((D,), jnp.float32), 'ln_b': jnp.zeros((D,), jnp.float32)}
    _L0_ffn_in = _L0_ffn_setup()
    _d = {'L0_attn_x': _L0_attn_in['x'], 'L0_attn_time_decay': _L0_attn_in['time_decay'], 'L0_attn_time_mix_k': _L0_attn_in['time_mix_k'], 'L0_attn_time_mix_v': _L0_attn_in['time_mix_v'], 'L0_attn_time_mix_r': _L0_attn_in['time_mix_r'], 'L0_attn_Wk': _L0_attn_in['Wk'], 'L0_attn_Wv': _L0_attn_in['Wv'], 'L0_attn_Wr': _L0_attn_in['Wr'], 'L0_attn_Wo': _L0_attn_in['Wo'], 'L0_attn_ln_g': _L0_attn_in['ln_g'], 'L0_attn_ln_b': _L0_attn_in['ln_b'], 'L0_ffn_ew': _L0_ffn_in['ew'], 'L0_ffn_act_w': _L0_ffn_in['act_w'], 'L0_ffn_We': _L0_ffn_in['We'], 'L0_ffn_be': _L0_ffn_in['be'], 'L0_ffn_Wq': _L0_ffn_in['Wq'], 'L0_ffn_Wk': _L0_ffn_in['Wk'], 'L0_ffn_Wv': _L0_ffn_in['Wv'], 'L0_ffn_Wo': _L0_ffn_in['Wo'], 'L0_ffn_ln_g': _L0_ffn_in['ln_g'], 'L0_ffn_ln_b': _L0_ffn_in['ln_b']}
    _x0 = _d['L0_attn_x']
    _d['L0_attn_x'] = jax.random.normal(jax.random.fold_in(jax.random.key(seed), 1), (4, 1024, 128), dtype=_x0.dtype)
    del _x0
    return _d

def reference(L0_attn_x, L0_attn_time_decay, L0_attn_time_mix_k, L0_attn_time_mix_v, L0_attn_time_mix_r, L0_attn_Wk, L0_attn_Wv, L0_attn_Wr, L0_attn_Wo, L0_attn_ln_g, L0_attn_ln_b, L0_ffn_ew, L0_ffn_act_w, L0_ffn_We, L0_ffn_be, L0_ffn_Wq, L0_ffn_Wk, L0_ffn_Wv, L0_ffn_Wo, L0_ffn_ln_g, L0_ffn_ln_b):

    def _L0_attn_ref(x, time_decay, time_mix_k, time_mix_v, time_mix_r, Wk, Wv, Wr, Wo, ln_g, ln_b):
        import jax, jax.numpy as jnp
        from jax import lax
        import numpy as np
        B, T, C = (8, 256, 128)
        ATT_SCALE = 1.0
        LN_EPS = 1e-05

        def _layernorm(x, g, b):
            mu = jnp.mean(x, axis=-1, keepdims=True)
            var = jnp.mean(jnp.square(x - mu), axis=-1, keepdims=True)
            return (x - mu) * lax.rsqrt(var + LN_EPS) * g + b

        def _wkv_scan(k, v, td):
            kT = jnp.swapaxes(k, 0, 1)
            vT = jnp.swapaxes(v, 0, 1)

            def step(carry, kv):
                num, den = carry
                kt, vt = kv
                den = den * td + kt
                num = num * td + kt * vt
                return ((num, den), num / (den + 1e-08))
            z = jnp.zeros((k.shape[0], k.shape[2]), dtype=k.dtype)
            _, wkvT = lax.scan(step, (z, z), (kT, vT))
            return jnp.swapaxes(wkvT, 0, 1)

        def _reference_tuple_inner(x, time_decay, time_mix_k, time_mix_v, time_mix_r, Wk, Wv, Wr, Wo, ln_g, ln_b):
            x = _layernorm(x, ln_g, ln_b)
            last_x = jnp.pad(x[:, :-1], ((0, 0), (1, 0), (0, 0)))
            k = (x * time_mix_k + last_x * (1.0 - time_mix_k)) @ Wk.T
            v = (x * time_mix_v + last_x * (1.0 - time_mix_v)) @ Wv.T
            r = (x * time_mix_r + last_x * (1.0 - time_mix_r)) @ Wr.T
            k = k * ATT_SCALE
            td = jnp.exp(time_decay)
            wkv = _wkv_scan(jnp.exp(k), v, td)
            out = jax.nn.sigmoid(r) * wkv @ Wo.T
            new_state = x[:, -1:]
            return (out, new_state)
        return _reference_tuple_inner(x, time_decay, time_mix_k, time_mix_v, time_mix_r, Wk, Wv, Wr, Wo, ln_g, ln_b)[0]

    def _L0_ffn_ref(inputs, ew, act_w, We, be, Wq, Wk, Wv, Wo, ln_g, ln_b):
        import jax, jax.numpy as jnp
        import numpy as np
        NUM_NOD = 6
        MAX_PREV = 5
        NUM_EDGE = 20
        D = 128
        H = 8
        LN_EPS = 1e-06

        def _layernorm(x, g, b):
            mu = jnp.mean(x, axis=-1, keepdims=True)
            var = jnp.mean(jnp.square(x - mu), axis=-1, keepdims=True)
            return (x - mu) * jax.lax.rsqrt(var + LN_EPS) * g + b

        def _mha(q, k, v, wq, wk, wv, wo):
            B, S, d = q.shape
            dh = d // H
            qh = (q @ wq).reshape(B, S, H, dh)
            kh = (k @ wk).reshape(B, S, H, dh)
            vh = (v @ wv).reshape(B, S, H, dh)
            scores = jnp.einsum('bqhd,bkhd->bhqk', qh, kh) / jnp.sqrt(jnp.asarray(dh, q.dtype))
            attn = jax.nn.softmax(scores, axis=-1)
            ctx = jnp.einsum('bhqk,bkhd->bqhd', attn, vh).reshape(B, S, d)
            return ctx @ wo
        nodes = {-1: inputs}
        lind = 0
        for c in range(NUM_NOD):
            nsrc = min(c + 1, MAX_PREV)
            snode = c - nsrc
            eq, ek, ev = (lind + nsrc - 1, lind, lind + nsrc // 2)
            in_q, in_k, in_v = (c - 1, snode, snode + nsrc // 2)
            q = ew[c, 0] * (nodes[in_q] @ We[eq] + be[eq])
            k = ew[c, 1] * (nodes[in_k] @ We[ek] + be[ek])
            v = ew[c, 2] * (nodes[in_v] @ We[ev] + be[ev])
            o = _mha(q, k, v, Wq[c], Wk[c], Wv[c], Wo[c])
            nodes[c] = act_w[c] * o + q
            lind += nsrc
        out = nodes[NUM_NOD - 1]
        return _layernorm(out, ln_g, ln_b)
    x = L0_attn_x
    x = x + _L0_attn_ref(_layernorm(x, axis=-1), L0_attn_time_decay, L0_attn_time_mix_k, L0_attn_time_mix_v, L0_attn_time_mix_r, L0_attn_Wk, L0_attn_Wv, L0_attn_Wr, L0_attn_Wo, L0_attn_ln_g, L0_attn_ln_b)
    x = x + _L0_ffn_ref(_layernorm(x, axis=-1), L0_ffn_ew, L0_ffn_act_w, L0_ffn_We, L0_ffn_be, L0_ffn_Wq, L0_ffn_Wk, L0_ffn_Wv, L0_ffn_Wo, L0_ffn_ln_g, L0_ffn_ln_b)
    return x

_drawn_inputs = setup_inputs


def setup_inputs(seed=0):
    import zlib

    import numpy as np

    out = dict(_drawn_inputs(seed))
    spreads = {'L0_attn_ln_g': (1.0, 0.2),
     'L0_attn_ln_b': (0.0, 0.1),
     'L0_ffn_be': (0.0, 0.1),
     'L0_ffn_ln_g': (1.0, 0.2),
     'L0_ffn_ln_b': (0.0, 0.1)}
    factors = {'L0_attn_time_mix_k': 2.954,
     'L0_attn_time_mix_r': 3.765,
     'L0_ffn_Wq': 64.0,
     'L0_ffn_Wk': 64.0}
    for name, (base, spread) in spreads.items():
        noise = np.random.default_rng([zlib.crc32(name.encode()), seed]).standard_normal(out[name].shape)
        drawn = base * np.exp(spread * noise) if base else spread * noise
        out[name] = jnp.asarray(drawn.astype(out[name].dtype))
    for name, factor in factors.items():
        out[name] = (out[name] * factor).astype(out[name].dtype)
    return out
```

```python
from contextlib import ExitStack

import concourse.bass as bass
from concourse import mybir

F32 = mybir.dt.float32
BF16 = mybir.dt.bfloat16
ALU = mybir.AluOpType
ACT = mybir.ActivationFunctionType
AX_X = mybir.AxisListType.X

P = 128
BANK = 512
NODES = 6
MAX_PREV = 5
H = 8
VW = 32
HG = P // VW
LOOKAHEAD = 2
E_SLOTS = 12
Q_SLOTS = (0, 0, 1, 1, 0, 2)
K_SLOTS = (0, 1, 0, 1, 2, 0)
LN_EPS = 1e-5
LN_EPS_OUT = 1e-6
WKV_EPS = 1e-8


class Signal:

    def __init__(self, handle):
        self.handle = handle
        self.count = 0

    def now(self):
        return (self, self.count)


class Queue:

    def __init__(self):
        self.steps = []

    def add(self, issue, waits=(), signal=None, by=1):
        if signal is not None:
            signal.count += by
        self.steps.append((issue, [w for w in waits if w is not None], signal, by))
        return None if signal is None else signal.now()

    def play(self, engine):
        reached = {}
        for issue, waits, signal, by in self.steps:
            for sig, value in waits:
                if reached.get(sig, 0) < value:
                    engine.wait_ge(sig.handle, value)
                    reached[sig] = value
            instruction = issue(engine) if issue is not None else None
            if signal is not None:
                instruction.then_inc(signal.handle, by)


def node_sources(c):
    first = sum(min(i + 1, MAX_PREV) for i in range(c))
    n = min(c + 1, MAX_PREV)
    return (first + n - 1, first, first + n // 2), (c - n, c - n + n // 2)


def build(nc, x, time_decay, mix_k, mix_v, mix_r, Wk, Wv, Wr, Wo, ln_g, ln_b, ew, act_w, We, be,
          fWq, fWk, fWv, fWo, fln_g, fln_b, out):
    B, S, D = x.shape
    DH = D // H
    NCH = S // P
    NHALF = S // BANK
    CPB = BANK // P
    assert D == P and DH * len(Q_SLOTS) + 3 <= P and H % HG == 0
    UNITS = NODES * B
    GPU = (H // HG) * NHALF
    GROUPS = UNITS * GPU
    SPLIT_ROWS = DH * len(Q_SLOTS)
    AUG_ROWS = SPLIT_ROWS + 3
    EXP_SCALE = DH ** -0.5
    SPILLED = NODES - 3

    pe, act, dve, pool, sp = Queue(), Queue(), Queue(), Queue(), Queue()
    ctx = ExitStack()
    with ctx:
        def sb(name, shape, dt=F32):
            return ctx.enter_context(nc.sbuf_tensor(name, shape, dt))

        signals = []

        def signal(name):
            s = Signal(ctx.enter_context(nc.semaphore(name)))
            signals.append(s)
            return s

        def dram(name, shape, dt=F32):
            return nc.dram_tensor(name, shape, dt, kind="Internal").ap()

        x2_dram = dram("x2_dram", [B, P, NCH, D])
        node_dram = dram("node_dram", [SPILLED + 1, B, P, S])
        part_dram = dram("part_dram", [2, 2, 3, P, S], BF16)
        max_dram = dram("max_dram", [2, 3, HG * CPB, P], BF16)
        den_dram = dram("den_dram", [2, H, S])
        rden_dram = dram("rden_dram", [2, H, S])

        node_ring = sb("node_ring", [P, B, 2, S])
        q_aug = sb("q_aug", [P, 2, H, S], BF16)
        k_aug = sb("k_aug", [P, 2, H, S], BF16)
        e_ring = sb("e_ring", [P, E_SLOTS, BANK])
        v_aug = sb("v_aug", [P, 2, NCH, H, VW])
        k_src = sb("k_src", [P, S])
        v_src = sb("v_src", [P, S])
        part = [sb("q_part", [P, 3, S], BF16), sb("k_part", [P, 3, S], BF16)]
        rest = [sb("q_rest", [P, S]), sb("k_rest", [P, S])]
        raw = sb("raw", [P, 2, BANK])
        ctxT = sb("ctxT", [P, S])
        rden_bc = sb("rden_bc", [P, S])
        den_pack = sb("den_pack", [P, H * S // P])
        rden_pack = sb("rden_pack", [P, H * S // P])
        w_edge_q = sb("w_edge_q", [P, NODES, D])
        w_q = sb("w_q", [P, NODES, D])
        w_o = sb("w_o", [P, NODES, D])
        w_k_fold = sb("w_k_fold", [P, NODES, D])
        w_v_fold = sb("w_v_fold", [P, NODES, D])
        v_bias = sb("v_bias", [P, NODES, D])
        col = sb("col", [P, 64])
        ident = sb("ident", [P, P])
        out_g = sb("out_g", [P, D])
        out_b = sb("out_b", [P, D])
        max_half = sb("max_half", [P, 2, HG * CPB, 2])
        max_col = sb("max_col", [P, 2, HG * CPB])
        max_rest = sb("max_rest", [HG * CPB, 2, P])
        max_part = sb("max_part", [HG * CPB, 2, 3, P], BF16)
        stats = sb("stats", [P, NCH, 6])
        meanvar = sb("meanvar", [P, NCH, 2])
        vareps = sb("vareps", [P, NCH])
        rstd = sb("rstd", [P, NCH])
        neg_half = sb("neg_half", [P, NCH])

        bank = [ctx.enter_context(nc.psum_tensor(f"bank{i}", [P, BANK], F32)) for i in range(8)]
        ST_BANKS, MAX_BANKS, CTX_BANK, MISC_BANK = (0, 1, 2), (3, 4, 5), 6, 7

        pe_st, pe_max, pe_ctx, pe_misc = (signal(n) for n in ("pe_st", "pe_max", "pe_ctx", "pe_misc"))
        act_exp, act_misc = signal("act_exp"), signal("act_misc")
        dve_max, dve_misc = signal("dve_max"), signal("dve_misc")
        pool_misc = signal("pool_misc")
        d_weights, d_x2_out, d_out = signal("d_weights"), signal("d_x2_out"), signal("d_out")
        d_x = [signal(f"d_x{b}") for b in range(B)]
        d_spill = [signal(f"d_spill{b}") for b in range(B)]
        d_part, d_aug = signal("d_part"), signal("d_aug")
        d_max_out = [signal(f"d_max_out{i}") for i in range(2)]
        d_max_in = [signal(f"d_max_in{i}") for i in range(2)]
        d_ctx = [signal(f"d_ctx{i}") for i in range(2)]
        d_den_in, d_rden_out, d_rden_in = signal("d_den_in"), signal("d_rden_out"), signal("d_rden_in")
        d_ksrc, d_vsrc, d_x2_in = signal("d_ksrc"), signal("d_vsrc"), signal("d_x2_in")

        bank_free = [None] * 8

        def dma(dst, src, sig, waits=()):
            return sp.add(lambda e: e.dma_start(dst, src), waits, sig, 16)

        def mm(dst, lhsT, rhs, waits=(), sig=None, start=True, stop=True):
            return pe.add(lambda e: e.matmul(dst, lhsT, rhs, start=start, stop=stop), waits, sig)

        def transpose(dst, src, waits=(), sig=None):
            return pe.add(lambda e: e.transpose(dst, src, ident[:, :]), waits, sig)

        def activate(dst, src, func, waits, bias=None, scale=None):
            kw = {}
            if bias is not None:
                kw["bias"] = bias
            if scale is not None:
                kw["scale"] = scale
            return act.add(lambda e: e.activation(dst, src, func, **kw), waits, act_misc)

        def vec(f, waits, sig=None):
            return dve.add(f, waits, sig or dve_misc)

        C_TD, C_MIX, C_OMM, C_LNG, C_LNB = 0, 1, 4, 7, 8
        C_EW, C_ACTW, C_BQ, C_BK, C_BE = 9, 27, 33, 39, 45

        def column(dst, src):
            return dma(dst, src.rearrange("(p a) -> p a", a=1), d_weights)

        def spread(dst, src, n):
            return dma(dst, src.rearrange("(a n) -> a n", a=1).to_broadcast([P, n]), d_weights)

        q_aug_f = q_aug[:, :, :, :].rearrange("p u h s -> p u (h s)").bitcast(F32)
        k_aug_f = k_aug[:, :, :, :].rearrange("p u h s -> p u (h s)").bitcast(F32)
        e_f = e_ring[:, :, :].rearrange("p n s -> p (n s)")
        x_nat = [e_f[:, b * S:(b + 1) * S] for b in range(B)]
        y_nat, t_a = e_f[:, B * S:(B + 1) * S], e_f[:, (B + 1) * S:(B + 2) * S]
        t_b, ek, ekv, er = (q_aug_f[:, 1, i * S:(i + 1) * S] for i in range(4))
        xT = k_aug_f[:, 1, 0:S + 1]
        t_c, t_d = (k_aug_f[:, 1, i * S:(i + 1) * S] for i in (2, 3))
        raw_w = q_aug_f[:, 0, :].rearrange("p (n d) -> p n d", d=D)
        WE_KV, W_KV, W_TIME = 0, 2 * NODES, 4 * NODES
        we_t = k_aug_f[:, 0, :].rearrange("p (n d) -> p n d", d=D)
        be_rows = k_aug_f[0:We.shape[0], 0, 30 * D:31 * D]
        be_rep = k_aug_f[:, 0, 28 * D:29 * D]
        w_time_t = rden_bc[:, 0:4 * D].rearrange("p (n d) -> p n d", d=D)

        for b in range(B):
            dma(x_nat[b].rearrange("p (k c) -> p k c", c=D), x[b].rearrange("(k p) c -> p k c", p=P), d_x[b])
            if b == 0:
                for i, w in enumerate((Wk, Wv, Wr, Wo)):
                    dma(raw_w[:, W_TIME + i, :], w, d_weights)
                column(col[:, C_TD:C_TD + 1], time_decay)
                for i, m in enumerate((mix_k, mix_v, mix_r)):
                    column(col[:, C_MIX + i:C_MIX + i + 1], m.rearrange("a b c -> (a b c)"))
                column(col[:, C_LNG:C_LNG + 1], ln_g)
                column(col[:, C_LNB:C_LNB + 1], ln_b)
        for c in range(NODES):
            (eq, ek_, ev), _ = node_sources(c)
            dma(w_edge_q[:, c, :], We[eq], d_weights)
            dma(raw_w[:, WE_KV + c, :], We[ek_], d_weights)
            dma(raw_w[:, WE_KV + NODES + c, :], We[ev], d_weights)
        for dst, src in ((raw_w[:, W_KV:W_KV + NODES, :], fWk), (raw_w[:, W_KV + NODES:W_KV + 2 * NODES, :], fWv),
                         (w_q[:, :, :], fWq), (w_o[:, :, :], fWo)):
            dma(dst, src.rearrange("n i o -> i n o"), d_weights)
        dma(be_rows, be, d_weights)
        spread(col[:, C_EW:C_EW + 3 * NODES], ew.rearrange("a b -> (a b)"), 3 * NODES)
        spread(col[:, C_ACTW:C_ACTW + NODES], act_w, NODES)
        spread(out_g[:, :], fln_g, D)
        spread(out_b[:, :], fln_b, D)
        weights_in = d_weights.now()

        pool.add(lambda e: e.memset(ident[:, :], 0.0), (), pool_misc)
        ident_done = pool.add(lambda e: e.affine_select(
            out=ident[:, :], in_=ident[:, :], compare_op=ALU.not_equal, fill=1.0, base=0,
            pattern=[[-1, P]], channel_multiplier=1), [pool_misc.now()], pool_misc)
        neg_half_done = pool.add(lambda e: e.memset(neg_half[:, :], -0.5), (), pool_misc)
        pool.add(lambda e: e.memset(v_aug[:, :, :, :, :].rearrange("p u c h w -> p (u c h w)"), 1.0), (), pool_misc)

        td_done = activate(col[:, C_TD:C_TD + 1], col[:, C_TD:C_TD + 1], ACT.Exp, [weights_in])
        omm_done = vec(lambda e: e.tensor_scalar(col[:, C_OMM:C_OMM + 3], col[:, C_MIX:C_MIX + 3], -1.0, 1.0,
                                                 ALU.mult, ALU.add), [weights_in])

        banks_used = [0]

        def fill_bank(first_waits, write, n):
            i = banks_used[0] % 8
            banks_used[0] += 1
            done = None
            for j in range(n):
                done = write(j, bank[i], [*first_waits, bank_free[i]] if j == 0 else (), pe_misc if j == n - 1 else None)
            return i, done

        def transpose_blocks(dst_of, src_of, n, waits, evacuate):
            for k in range(0, n, CPB):
                m = min(CPB, n - k)
                i, done = fill_bank(waits, lambda j, bk, w, s: transpose(bk[:, j * P:(j + 1) * P], src_of(k + j), w, s), m)
                bank_free[i] = evacuate(dst_of(k, m), bank[i][:, 0:m * P], done)
            return bank_free[i]

        def act_copy(dst, src, done):
            return activate(dst, src, ACT.Copy, [done])

        time_w_done = transpose_blocks(
            lambda k, m: w_time_t[:, k:k + m, :].rearrange("p n d -> p (n d)"),
            lambda j: raw_w[:, W_TIME + j, :], 4, [ident_done, weights_in], act_copy)
        edge_done = transpose_blocks(
            lambda k, m: we_t[:, k:k + m, :].rearrange("p n d -> p (n d)"),
            lambda j: raw_w[:, WE_KV + j, :], 2 * NODES, [ident_done, weights_in], act_copy)
        i, done = fill_bank([weights_in], lambda j, bk, w, s: pe.add(lambda e: e.transpose(
            bk[:, 0:We.shape[0]], be_rows, ident[0:We.shape[0], 0:We.shape[0]]), w, s), 1)
        be_cols = we_t[:, 24, 0:We.shape[0]]
        bank_free[i] = be_done = activate(be_cols, bank[i][:, 0:We.shape[0]], ACT.Copy, [done])

        for c in range(NODES):
            (eq, ek_, ev), _ = node_sources(c)
            ewq, ewk, ewv = (col[:, C_EW + 3 * c + i:C_EW + 3 * c + i + 1] for i in range(3))

            def fold(j, bk, w, s, c=c):
                return mm(bk[:, j * P:(j + 1) * P], we_t[:, j * NODES + c, :], raw_w[:, W_KV + j * NODES + c, :], w, s)
            i, done = fill_bank([edge_done], fold, 2)
            vec(lambda e, i=i, c=c, s=ewk: e.tensor_scalar(w_k_fold[:, c, :], bank[i][:, 0:P], s, None, ALU.mult), [done])
            bank_free[i] = vec(lambda e, i=i, c=c, s=ewv: e.tensor_scalar(
                w_v_fold[:, c, :], bank[i][:, P:2 * P], s, None, ALU.mult), [done])
            i, done = fill_bank([be_done], lambda j, bk, w, s, c=c, ek_=ek_: mm(
                bk[:, 0:1], raw_w[:, W_KV + c, :], be_cols[:, ek_:ek_ + 1], w, s), 1)
            bank_free[i] = vec(lambda e, i=i, c=c, s=ewk: e.tensor_scalar(
                col[:, C_BK + c:C_BK + c + 1], bank[i][:, 0:1], s, None, ALU.mult), [done])
            rep_done = vec(lambda e, ev=ev: e.tensor_copy(be_rep, be_cols[:, ev:ev + 1].to_broadcast([P, P])),
                           [be_done, pe_misc.now()])
            i, done = fill_bank([rep_done], lambda j, bk, w, s, c=c: mm(
                bk[:, 0:P], be_rep, raw_w[:, W_KV + NODES + c, :], w, s), 1)
            bank_free[i] = vec(lambda e, i=i, c=c, s=ewv: e.tensor_scalar(
                v_bias[:, c, :], bank[i][:, 0:P], s, None, ALU.mult), [done])
            vec(lambda e, c=c, s=ewq, eq=eq: e.tensor_scalar(col[:, C_BQ + c:C_BQ + c + 1], be_cols[:, eq:eq + 1], s,
                                                             None, ALU.mult), [be_done])
            pool.add(lambda e, c=c, s=ewq: e.tensor_scalar(w_edge_q[:, c, :], w_edge_q[:, c, :], s, None, ALU.mult),
                     [weights_in], pool_misc)
            pool.add(lambda e, c=c: e.tensor_scalar(w_o[:, c, :], w_o[:, c, :], col[:, C_ACTW + c:C_ACTW + c + 1],
                                                    None, ALU.mult), [weights_in], pool_misc)

        def layernorm_nat(dst, src, eps, waits):
            s3 = src.rearrange("p (k c) -> p k c", c=D)
            d3 = dst.rearrange("p (k c) -> p k c", c=D)
            for k in range(NCH):
                done = vec(lambda e, k=k: e.bn_stats(stats[:, k, :], s3[:, k, :]), waits)
            for k in range(NCH):
                done2 = vec(lambda e, k=k: e.bn_aggr(meanvar[:, k, :], stats[:, k, :]), [done, pool_misc.now()])
            done = vec(lambda e: e.tensor_scalar(vareps[:, :], meanvar[:, :, 1], eps, None, ALU.add), [done2])
            done = pool.add(lambda e: e.tensor_tensor(rstd[:, :], vareps[:, :], neg_half[:, :], ALU.pow),
                            [done, neg_half_done], pool_misc)
            for k in range(NCH):
                last = vec(lambda e, k=k: e.tensor_scalar(d3[:, k, :], s3[:, k, :], meanvar[:, k, 0:1], rstd[:, k:k + 1],
                                                          ALU.subtract, ALU.mult), [done])
            return last

        node_ready = [None] * B
        for b in range(B):
            y_done = layernorm_nat(y_nat, x_nat[b], LN_EPS, [d_x[b].now(), pe_misc.now()])
            y_done = layernorm_nat(y_nat, y_nat, LN_EPS, [y_done])
            pad_done = vec(lambda e: e.memset(xT[:, 0:1], 0.0), [pe_misc.now()])
            xT_done = transpose_blocks(
                lambda k, m: xT[:, 1 + k * P:1 + (k + m) * P], lambda j: y_nat[:, j * P:(j + 1) * P], NCH,
                [y_done, ident_done],
                lambda dst, src, done: activate(dst, src, ACT.Identity, [done, pad_done],
                                                bias=col[:, C_LNB:C_LNB + 1], scale=col[:, C_LNG:C_LNG + 1]))
            ready = {}
            for n, name in enumerate("kvr"):
                last_part, mixed = ((t_a, t_b), (t_c, t_d))[n % 2]
                mix, omm = (col[:, cc + n:cc + n + 1] for cc in (C_MIX, C_OMM))
                done = pool.add(lambda e, d=last_part, m=omm: e.tensor_scalar(d, xT[:, 0:S], m, None, ALU.mult),
                                [xT_done, pad_done, omm_done, pe_misc.now(), dve_misc.now()], pool_misc)
                mixed_done = vec(lambda e, d=mixed, a=last_part, m=mix: e.scalar_tensor_tensor(
                    out=d, in0=xT[:, 1:S + 1], scalar=m, in1=a, op0=ALU.mult, op1=ALU.add), [done, xT_done, pe_misc.now()])
                for hf in range(NHALF):
                    cols = slice(hf * BANK, (hf + 1) * BANK)
                    i, done = fill_bank([mixed_done, time_w_done], lambda j, bk, w, s, n=n, mixed=mixed, cols=cols: mm(
                        bk[:, :], w_time_t[:, n, :], mixed[:, cols], w, s), 1)
                    if name == "k":
                        bank_free[i] = activate(ek[:, cols], bank[i][:, :], ACT.Exp, [done, dve_misc.now()])
                        ready["k"] = bank_free[i]
                    elif name == "v":
                        bank_free[i] = vec(lambda e, i=i, cols=cols: e.tensor_tensor(
                            ekv[:, cols], bank[i][:, :], ek[:, cols], ALU.mult), [done, ready["k"]])
                        ready["v"] = bank_free[i]
                    else:
                        bank_free[i] = activate(er[:, cols], bank[i][:, :], ACT.Exp, [done, dve_misc.now()], scale=-1.0)
                        ready["r"] = bank_free[i]
            er1_done = pool.add(lambda e: e.tensor_scalar(er, er, 1.0, None, ALU.add), [ready["r"]], pool_misc)
            td = col[:, C_TD:C_TD + 1].to_broadcast([P, S])
            den, num, prod, rec, gated = y_nat, t_c, t_d, t_a, ekv
            den_done = vec(lambda e: e.tensor_tensor_scan(den, td, ek, 0.0, ALU.mult, ALU.add),
                           [td_done, ready["k"], pe_misc.now()])
            num_done = vec(lambda e: e.tensor_tensor_scan(num, td, ekv, 0.0, ALU.mult, ALU.add), [ready["v"], pe_misc.now()])
            done = vec(lambda e: e.scalar_tensor_tensor(out=prod, in0=den, scalar=WKV_EPS, in1=er, op0=ALU.add, op1=ALU.mult),
                       [den_done, er1_done, pe_misc.now()])
            rec_done = vec(lambda e: e.reciprocal(rec, prod), [done])
            gated_done = pool.add(lambda e: e.tensor_tensor(gated, num, rec, ALU.mult), [rec_done, num_done], pool_misc)
            for k in range(0, NCH, CPB):
                i, done = fill_bank([gated_done], lambda j, bk, w, s, k=k: mm(
                    bk[:, j * P:(j + 1) * P], gated[:, (k + j) * P:(k + j + 1) * P], w_time_t[:, 3, :], w, s), CPB)
                xs = x_nat[b][:, k * P:(k + CPB) * P]
                bank_free[i] = x2_done = vec(lambda e, i=i, xs=xs: e.tensor_tensor(xs, bank[i][:, :], xs, ALU.add), [done])
            dma(x2_dram[b], x_nat[b].rearrange("p (k c) -> p k c", c=D), d_x2_out, [x2_done])
            f_done = layernorm_nat(y_nat, x_nat[b], LN_EPS, [x2_done])
            node_ready[b] = transpose_blocks(
                lambda k, m: node_ring[:, b, 0, k * P:(k + m) * P], lambda j: y_nat[:, j * P:(j + 1) * P], NCH,
                [f_done], act_copy)
            dma(node_dram[0, b], node_ring[:, b, 0, :], d_spill[b], [node_ready[b]])

        prologue_done = [s.now() for s in signals if s.count]
        ones_done = pool.add(lambda e: e.memset(k_aug[SPLIT_ROWS:AUG_ROWS, :, :, :].rearrange("p u h s -> p (u h s)"), 1.0),
                             prologue_done, pool_misc)
        for q in (pe, act, dve, sp):
            q.add(None, prologue_done + [ones_done])

        counts = dict(st=0, mx=0, e=0)
        st_free = [None] * len(ST_BANKS)
        max_free = [None] * len(MAX_BANKS)
        misc_free, ctx_free = [None], [None]
        e_free = [None] * E_SLOTS
        aug_in, part_out = {}, {}
        max_rows_in = {}
        v_ready, v_read = {}, {}
        ctx_moved = {}
        last_st = {}

        def misc_fill(waits, write, n=1):
            done = None
            for j in range(n):
                done = write(j, bank[MISC_BANK], [*waits, misc_free[0]] if j == 0 else (), pe_misc if j == n - 1 else None)
            return done

        k_read, x2_read = [None], [None]

        def load_k_source(u):
            c, b = divmod(u, B)
            dma(k_src[:, :], node_dram[node_sources(c)[1][0] + 1, b], d_ksrc, [d_spill[b].now(), k_read[0], x2_read[0]])

        def load_v_source(u):
            c, b = divmod(u, B)
            dma(v_src[:, :], node_dram[node_sources(c)[1][1] + 1, b], d_vsrc, [d_spill[b].now(), pe_misc.now()])

        def project_q(u, hf):
            c, b = divmod(u, B)
            cols = slice(hf * BANK, (hf + 1) * BANK)
            done = misc_fill([node_ready[b]], lambda j, bk, w, s: mm(bk[:, :], w_edge_q[:, c, :], node_ring[:, b, c % 2, cols], w, s))
            misc_free[0] = activate(node_ring[:, b, (c + 1) % 2, cols], bank[MISC_BANK][:, :], ACT.Identity,
                                    [done, d_spill[b].now()], bias=col[:, C_BQ + c:C_BQ + c + 1])
            return misc_free[0]

        q_done = {}
        split_done = {}

        def project_head(u, side, hf):
            c, b = divmod(u, B)
            cols = slice(hf * BANK, (hf + 1) * BANK)
            w_, src, ready = ((w_q, node_ring[:, b, (c + 1) % 2, cols], q_done.get((u, hf))),
                              (w_k_fold, k_src[:, cols], d_ksrc.now()))[side]
            done = misc_fill([ready], lambda j, bk, w, s: mm(bk[:, :], w_[:, c, :], src, w, s))
            if side == 1:
                k_read[0] = done
            p1 = part[side][:, 0, cols]
            bias = col[:, C_BK + c:C_BK + c + 1]
            if side == 0:
                p1_done = activate(p1, bank[MISC_BANK][:, :], ACT.Copy, [done, d_part.now()])
            else:
                p1_done = activate(p1, bank[MISC_BANK][:, :], ACT.Identity, [done, d_part.now()], bias=bias)
            split_done[u, side, hf, 1] = p1_done

        def split_rest(u, side, hf):
            c, _ = divmod(u, B)
            cols = slice(hf * BANK, (hf + 1) * BANK)
            p1, r = part[side][:, 0, cols], rest[side][:, cols]
            bias = 0.0 if side == 0 else col[:, C_BK + c:C_BK + c + 1]
            waits = [split_done[u, side, hf, 1], pool_misc.now()]
            if side == 0:
                misc_free[0] = vec(lambda e: e.tensor_tensor(r, bank[MISC_BANK][:, :], p1, ALU.subtract), waits)
            else:
                misc_free[0] = vec(lambda e: e.scalar_tensor_tensor(
                    out=r, in0=bank[MISC_BANK][:, :], scalar=bias, in1=p1, op0=ALU.add, op1=ALU.subtract), waits)
            split_done[u, side, hf, 2] = misc_free[0]

        def split_low(u, side):
            r, p2, p3 = rest[side][:, :], part[side][:, 1, :], part[side][:, 2, :]
            done = act.add(lambda e: e.activation(p2, r, ACT.Copy), [split_done[u, side, 1, 2]], act_misc)
            split_done[u, side] = pool.add(lambda e: e.tensor_tensor(p3, r, p2, ALU.subtract), [done], pool_misc)

        def store_parts(u, side):
            waits = [split_done[u, side]]
            for p in range(3):
                part_out[u] = dma(part_dram[u % 2, side, p], part[side][:, p, :], d_part, waits)

        def load_aug(u):
            waits = [part_out[u], last_st.get(u - 2)]
            for side, (aug, slots) in enumerate(((q_aug, Q_SLOTS), (k_aug, K_SLOTS))):
                for i, p in enumerate(slots):
                    aug_in[u] = dma(aug[i * DH:(i + 1) * DH, u % 2, :, :],
                                    part_dram[u % 2, side, p].rearrange("(h d) s -> d h s", d=DH), d_aug, waits)

        def project_v(u, hf):
            c, _ = divmod(u, B)
            k0 = hf * CPB
            done = misc_fill([d_vsrc.now()], lambda j, bk, w, s: mm(
                bk[:, j * P:(j + 1) * P], v_src[:, (k0 + j) * P:(k0 + j + 1) * P], w_v_fold[:, c, :], w, s), CPB)
            bias = v_bias[:, c, :].rearrange("p (o h d) -> p o h d", o=1, h=H).to_broadcast([P, CPB, H, DH])
            misc_free[0] = v_ready[u] = vec(lambda e: e.tensor_tensor(
                v_aug[:, u % 2, k0:k0 + CPB, :, 0:DH],
                bank[MISC_BANK][:, :].rearrange("p (k h d) -> p k h d", k=CPB, h=H), bias, ALU.add),
                [done, v_read.get(u - 2)])

        def max_rows(G):
            u, g = divmod(G, GPU)
            hg, qh = divmod(g, NHALF)
            r = G % 2
            NR = HG * CPB
            state = {}

            def combine():
                state["col"] = combined[G] = vec(lambda e: e.tensor_reduce(max_col[:, r, :], max_half[:, r, :, :], AX_X, ALU.max), [dve_max.now()])
                i = state["i"] = counts["mx"] % len(MAX_BANKS)
                counts["mx"] += 1
                state["t"] = pe.add(lambda e: e.transpose(bank[MAX_BANKS[i]][0:NR, 0:P], max_col[:, r, :], ident[:, :]),
                                    [state["col"], max_free[i]], pe_max)

            def split():
                i = state["i"]
                src = bank[MAX_BANKS[i]][0:NR, 0:P]
                p = [max_part[:, r, i, :] for i in range(3)]
                a = vec(lambda e: e.tensor_scalar(p[0], src, -1.0, None, ALU.mult),
                        [state["t"], d_max_out[r].now()])
                b_ = max_free[i] = vec(lambda e: e.scalar_tensor_tensor(
                    out=max_rest[:, r, :], in0=src, scalar=-1.0, in1=p[0], op0=ALU.mult, op1=ALU.subtract), [a])
                c_ = vec(lambda e: e.tensor_copy(p[1], max_rest[:, r, :]), [b_])
                state["s"] = vec(lambda e: e.tensor_tensor(p[2], max_rest[:, r, :], p[1], ALU.subtract), [c_])

            def move():
                o = dma(max_dram[r].rearrange("i n s -> n i s"), max_part[:, r, :, :], d_max_out[r], [state["s"]])
                max_rows_in[G] = dma(
                    q_aug[SPLIT_ROWS:AUG_ROWS, u % 2, hg * HG:(hg + 1) * HG, qh * BANK:(qh + 1) * BANK],
                    max_dram[r].rearrange("i (h t) s -> i h (t s)", h=HG), d_max_in[r], [o, last_st.get(u - 2)])
            return combine, split, move

        def evacuate_ctx(G, pv_done):
            u, g = divmod(G, GPU)
            hg, qh = divmod(g, NHALF)
            r = G % 2
            ctx_free[0] = done = activate(raw[:, r, :], bank[CTX_BANK][:, :], ACT.Copy, [pv_done, d_ctx[r].now()])

            def move():
                cols = slice(qh * BANK, (qh + 1) * BANK)
                for j in range(HG):
                    h = hg * HG + j
                    dma(ctxT[h * DH:(h + 1) * DH, cols], raw[j * VW:j * VW + DH, r, :], d_ctx[r], [done, out_read.get(u - 1)])
                ctx_moved[G] = dma(den_dram[u % 2, hg * HG:(hg + 1) * HG, cols], raw[DH:P:VW, r, :], d_ctx[r], [done])
            return move

        out_read = {}

        def finish_unit(u):
            c, b = divmod(u, B)
            state = {}

            def load_den():
                dma(den_pack[:, :], den_dram[u % 2].rearrange("h (a s) -> (h a) s", s=H * S // P), d_den_in,
                    [ctx_moved[u * GPU + g] for g in range(GPU)])

            def reciprocal():
                state["r"] = vec(lambda e: e.reciprocal(rden_pack[:, :], den_pack[:, :]), [d_den_in.now(), d_rden_out.now()])

            def spread_rden():
                o = dma(rden_dram[u % 2].rearrange("h (a s) -> (h a) s", s=H * S // P), rden_pack[:, :], d_rden_out, [state["r"]])
                for h in range(H):
                    dma(rden_bc[h * DH:(h + 1) * DH, :], rden_dram[u % 2, h:h + 1, :].to_broadcast([DH, S]), d_rden_in,
                        [o, pool_misc.now(), dve_misc.now()])

            def normalise():
                state["n"] = pool.add(lambda e: e.tensor_tensor(ctxT[:, :], ctxT[:, :], rden_bc[:, :], ALU.mult),
                                      [d_rden_in.now(), ctx_moved[u * GPU + GPU - 1], ctx_moved[u * GPU + GPU - 2]], pool_misc)

            def project(hf):
                def run():
                    cols = slice(hf * BANK, (hf + 1) * BANK)
                    node = node_ring[:, b, (c + 1) % 2, cols]
                    done = misc_fill([state["n"]], lambda j, bk, w, s: mm(bk[:, :], w_o[:, c, :], ctxT[:, cols], w, s))
                    misc_free[0] = node_ready[b] = vec(lambda e: e.tensor_tensor(node, bank[MISC_BANK][:, :], node, ALU.add), [done])
                    out_read[u] = done
                return run

            def spill():
                if c < SPILLED:
                    dma(node_dram[c + 1, b], node_ring[:, b, (c + 1) % 2, :], d_spill[b], [node_ready[b]])
            stages = {3: [load_den], 4: [reciprocal], 5: [spread_rden], 7: [normalise], 9: [project(0)], 10: [project(1)]}
            stages.update(finish_batch(u) if c == NODES - 1 else {11: [spill]})
            return stages

        def finish_batch(u):
            c, b = divmod(u, B)
            y, x2 = rden_bc, k_src
            yb = y[:, :]
            state = {}

            def turn(hf):
                def run():
                    k0 = hf * CPB
                    done = misc_fill([node_ready[b]], lambda j, bk, w, s: transpose(
                        bk[:, j * P:(j + 1) * P], node_ring[:, b, (c + 1) % 2, (k0 + j) * P:(k0 + j + 1) * P], w, s), CPB)
                    misc_free[0] = state["y"] = activate(y[:, k0 * P:(k0 + CPB) * P], bank[MISC_BANK][:, :], ACT.Copy, [done])
                    if hf == 0:
                        dma(x2[:, :].rearrange("p (k c) -> p k c", c=D), x2_dram[b], d_x2_in, [k_read[0]])
                return run

            def norm():
                state["n"] = layernorm_nat(yb, yb, LN_EPS_OUT, [state["y"]])

            def affine():
                y3 = yb.rearrange("p (k c) -> p k c", c=D)
                g3, b3 = (t[:, :].rearrange("p (o c) -> p o c", o=1).to_broadcast([P, NCH, D]) for t in (out_g, out_b))
                a = pool.add(lambda e: e.tensor_tensor(y3, y3, g3, ALU.mult), [state["n"]], pool_misc)
                a = pool.add(lambda e: e.tensor_tensor(y3, y3, b3, ALU.add), [a], pool_misc)
                state["o"] = x2_read[0] = pool.add(lambda e: e.tensor_tensor(yb, yb, x2[:, :], ALU.add), [a, d_x2_in.now()],
                                                   pool_misc)

            def store():
                dma(out[b].rearrange("(k p) c -> p k c", p=P), yb.rearrange("p (k c) -> p k c", c=D), d_out, [state["o"]])
            return {12: [turn(0)], 13: [turn(1)], 14: [norm], 16: [affine], 19: [store]}

        def projection_stages(u):
            def q(hf):
                def run():
                    q_done[u, hf] = project_q(u, hf)
                return run
            return {1: [q(0)], 2: [q(1)],
                    3: [lambda: project_head(u, 1, 0), lambda: split_rest(u, 1, 0)],
                    4: [lambda: project_head(u, 1, 1), lambda: split_rest(u, 1, 1)],
                    5: [lambda: (split_low(u, 1), project_head(u, 0, 0)), lambda: split_rest(u, 0, 0)],
                    6: [lambda: (store_parts(u, 1), project_head(u, 0, 1)), lambda: split_rest(u, 0, 1)],
                    7: [lambda: split_low(u, 0)], 8: [lambda: store_parts(u, 0)], 9: [lambda: load_aug(u)]}

        def score_tile(G, chunk, j):
            u, g = divmod(G, GPU)
            hg, qh = divmod(g, NHALF)
            h = hg * HG + j
            n = counts["st"]
            counts["st"] += 1
            i = n % len(ST_BANKS)
            last_st[u] = done = mm(bank[ST_BANKS[i]][:, :], k_aug[0:AUG_ROWS, u % 2, h, chunk * P:(chunk + 1) * P],
                                   q_aug[0:AUG_ROWS, u % 2, h, qh * BANK:(qh + 1) * BANK],
                                   [st_free[i], max_rows_in[G], aug_in[u]], pe_st)
            st_free[i] = act.add(lambda e: e.activation(e_ring[:, n % E_SLOTS, :], bank[ST_BANKS[i]][:, :], ACT.Exp, scale=EXP_SCALE),
                                 [done, e_free[n % E_SLOTS]], act_exp)
            return n % E_SLOTS, st_free[i]

        def max_tile(G, t):
            u, g = divmod(G, GPU)
            hg, qh = divmod(g, NHALF)
            row, kh = divmod(t, NHALF)
            j, qt = divmod(row, CPB)
            h = hg * HG + j
            q0 = qh * BANK + qt * P
            i = counts["mx"] % len(MAX_BANKS)
            counts["mx"] += 1
            done = mm(bank[MAX_BANKS[i]][:, :], q_aug[0:SPLIT_ROWS, u % 2, h, q0:q0 + P],
                      k_aug[0:SPLIT_ROWS, u % 2, h, kh * BANK:(kh + 1) * BANK], [max_free[i], aug_in[u]], pe_max)
            max_free[i] = dve.add(lambda e: e.tensor_reduce(max_half[:, G % 2, row, kh:kh + 1], bank[MAX_BANKS[i]][:, :],
                                                            AX_X, ALU.max), [done, combined.get(G - 2)], dve_max)

        combined = {}

        def context(G, chunk, tiles):
            u, g = divmod(G, GPU)
            hg = g // NHALF
            for j, (slot, ready) in enumerate(tiles):
                done = mm(bank[CTX_BANK][j * VW:(j + 1) * VW, :], v_aug[:, u % 2, chunk, hg * HG + j, :], e_ring[:, slot, :],
                          [ready, v_ready[u], ctx_free[0] if chunk == 0 else None], pe_ctx if j == HG - 1 else None,
                          start=(chunk == 0), stop=(chunk == NCH - 1))
            for slot, _ in tiles:
                e_free[slot] = done
            v_read[u] = done
            return done

        due = {}

        def schedule(at, stages):
            for chunk, halves in stages.items():
                for k, stage in enumerate(halves):
                    due.setdefault(2 * (at + chunk) + k, []).append(stage)

        UNIT_CHUNKS = GPU * NCH
        MAX_TILES = HG * CPB * NHALF // NCH

        load_k_source(0)
        load_v_source(0)
        for halves in projection_stages(0).values():
            for stage in halves:
                stage()
        for hf in range(NHALF):
            project_v(0, hf)

        for u in range(UNITS):
            if u > 0:
                slot = (u - 1) * UNIT_CHUNKS
                schedule(slot, {0: [lambda u=u: load_k_source(u)], 16: [lambda u=u: load_v_source(u)],
                                18: [lambda u=u: project_v(u, 0)], 19: [lambda u=u: project_v(u, 1)]})
                schedule(slot, projection_stages(u))
            schedule((u + 1) * UNIT_CHUNKS, finish_unit(u))

        previous = None
        last_step = (UNITS + 1) * UNIT_CHUNKS
        for step in range(-LOOKAHEAD * NCH, last_step):
            G, chunk = divmod(step, NCH)
            tiles = []
            for j in range(HG):
                if 0 <= G < GROUPS:
                    tiles.append(score_tile(G, chunk, j))
                if G + LOOKAHEAD < GROUPS:
                    max_tile(G + LOOKAHEAD, chunk * MAX_TILES + j)
                if j % 2:
                    for stage in due.pop(2 * step + j // 2, ()):
                        stage()
            if previous is not None:
                done = context(*previous)
                if previous[1] == NCH - 1:
                    schedule(step + 1, {0: [evacuate_ctx(previous[0], done)]})
            previous = (G, chunk, tiles) if tiles else None
            if chunk == NCH - 1 and G + LOOKAHEAD < GROUPS:
                combine, split, move = max_rows(G + LOOKAHEAD)
                schedule(step + 1, {0: [combine, split], 1: [move]})
        assert not due, sorted(due)

        sp.add(None, [s.now() for s in signals if s.count])

        with nc.Block() as block:
            @block.tensor
            def _(e):
                pe.play(e)

            @block.scalar
            def _(e):
                act.play(e)

            @block.vector
            def _(e):
                dve.play(e)

            @block.gpsimd
            def _(e):
                pool.play(e)

            @block.sync
            def _(e):
                sp.play(e)


_INS = ["L0_attn_x", "L0_attn_time_decay", "L0_attn_time_mix_k", "L0_attn_time_mix_v", "L0_attn_time_mix_r",
        "L0_attn_Wk", "L0_attn_Wv", "L0_attn_Wr", "L0_attn_Wo", "L0_attn_ln_g", "L0_attn_ln_b", "L0_ffn_ew",
        "L0_ffn_act_w", "L0_ffn_We", "L0_ffn_be", "L0_ffn_Wq", "L0_ffn_Wk", "L0_ffn_Wv", "L0_ffn_Wo",
        "L0_ffn_ln_g", "L0_ffn_ln_b"]


def kernel(**inputs):
    import numpy as _np
    import concourse.bacc as _bacc
    from concourse import mybir as _mybir
    from concourse.bass_utils import run_bass_kernel_spmd as _run

    nc = _bacc.Bacc("TRN2", target_bir_lowering=False, num_devices=1)
    arrays, args = {}, []
    for name in _INS:
        a = _np.ascontiguousarray(inputs[name])
        arrays[f"in_{name}"] = a
        args.append(nc.dram_tensor(f"in_{name}", a.shape, _mybir.dt.from_np(a.dtype), kind="ExternalInput").ap())
    out = nc.dram_tensor("out_0", arrays["in_L0_attn_x"].shape, F32, kind="ExternalOutput").ap()
    build(nc, *args, out)
    r = _run(nc, [arrays], core_ids=[0])
    return r.results[0]["out_0"]
```

```python
from contextlib import ExitStack

import concourse.bass as bass
from concourse import mybir

F32 = mybir.dt.float32
BF16 = mybir.dt.bfloat16
ALU = mybir.AluOpType
ACT = mybir.ActivationFunctionType
AX_X = mybir.AxisListType.X

P = 128
BANK = 512
NODES = 6
MAX_PREV = 5
H = 8
VW = 32
HG = P // VW
LOOKAHEAD = 2
E_SLOTS = 10
Q_SLOTS = (0, 0, 1, 1, 0, 2)
K_SLOTS = (0, 1, 0, 1, 2, 0)
LN_EPS = 1e-5
LN_EPS_OUT = 1e-6
WKV_EPS = 1e-8


class Signal:

    def __init__(self, handle):
        self.handle = handle
        self.count = 0

    def now(self):
        return (self, self.count)


class Queue:

    def __init__(self):
        self.steps = []

    def add(self, issue, waits=(), signal=None, by=1):
        if signal is not None:
            signal.count += by
        self.steps.append((issue, [w for w in waits if w is not None], signal, by))
        return None if signal is None else signal.now()

    def play(self, engine):
        reached = {}
        for issue, waits, signal, by in self.steps:
            for sig, value in waits:
                if reached.get(sig, 0) < value:
                    engine.wait_ge(sig.handle, value)
                    reached[sig] = value
            instruction = issue(engine) if issue is not None else None
            if signal is not None:
                instruction.then_inc(signal.handle, by)


def node_sources(c):
    first = sum(min(i + 1, MAX_PREV) for i in range(c))
    n = min(c + 1, MAX_PREV)
    return (first + n - 1, first, first + n // 2), (c - n, c - n + n // 2)


def build(nc, x, time_decay, mix_k, mix_v, mix_r, Wk, Wv, Wr, Wo, ln_g, ln_b, ew, act_w, We, be,
          fWq, fWk, fWv, fWo, fln_g, fln_b, out):
    B, S, D = x.shape
    DH = D // H
    NCH = S // P
    NHALF = S // BANK
    CPB = BANK // P
    assert D == P and DH * len(Q_SLOTS) + 3 <= P and H % HG == 0
    UNITS = NODES * B
    GPU = (H // HG) * NHALF
    GROUPS = UNITS * GPU
    SPLIT_ROWS = DH * len(Q_SLOTS)
    AUG_ROWS = SPLIT_ROWS + 3
    EXP_SCALE = DH ** -0.5
    SPILLED = NODES - 3

    pe, act, dve, pool, sp = Queue(), Queue(), Queue(), Queue(), Queue()
    ctx = ExitStack()
    with ctx:
        def sb(name, shape, dt=F32):
            return ctx.enter_context(nc.sbuf_tensor(name, shape, dt))

        signals = []

        def signal(name):
            s = Signal(ctx.enter_context(nc.semaphore(name)))
            signals.append(s)
            return s

        def dram(name, shape, dt=F32):
            return nc.dram_tensor(name, shape, dt, kind="Internal").ap()

        x2_dram = dram("x2_dram", [B, P, NCH, D])
        node_dram = dram("node_dram", [SPILLED + 1, B, P, S])
        part_dram = dram("part_dram", [2, 2, 3, P, S], BF16)
        max_dram = dram("max_dram", [2, 3, HG * CPB, P], BF16)
        den_dram = dram("den_dram", [2, H, S])
        rden_dram = dram("rden_dram", [2, H, S])

        node_ring = sb("node_ring", [P, B, 2, S])
        q_aug = sb("q_aug", [P, 2, H, S], BF16)
        k_aug = sb("k_aug", [P, 2, H, S], BF16)
        e_ring = sb("e_ring", [P, E_SLOTS, BANK])
        v_aug = sb("v_aug", [P, 2, NCH, H, VW])
        src = sb("src", [P, S])
        part = [sb("q_part", [P, 3, S], BF16), sb("k_part", [P, 3, S], BF16)]
        rest = sb("rest", [P, S])
        raw = sb("raw", [P, 2, BANK])
        ctxT = sb("ctxT", [P, S])
        rden_bc = sb("rden_bc", [P, S])
        den_pack = sb("den_pack", [P, H * S // P])
        rden_pack = sb("rden_pack", [P, H * S // P])
        w_edge_q = sb("w_edge_q", [P, NODES, D])
        w_q = sb("w_q", [P, NODES, D])
        w_o = sb("w_o", [P, NODES, D])
        w_k_fold = sb("w_k_fold", [P, NODES, D])
        w_v_fold = sb("w_v_fold", [P, NODES, D])
        v_bias = sb("v_bias", [P, NODES, D])
        col = sb("col", [P, 64])
        ident = sb("ident", [P, P])
        carried_col = sb("carried_col", [P, 2, 2])
        out_g = sb("out_g", [P, D])
        out_b = sb("out_b", [P, D])
        max_half = sb("max_half", [P, 2, HG * CPB, 2])
        max_col = sb("max_col", [P, 2, HG * CPB])
        max_neg = sb("max_neg", [HG * CPB, 2, P])
        max_rest = sb("max_rest", [HG * CPB, 2, P])
        max_part = sb("max_part", [HG * CPB, 2, 3, P], BF16)
        stats = sb("stats", [P, 5, CPB, 6])
        meanvar = sb("meanvar", [P, 5, CPB, 2])
        vareps = sb("vareps", [P, 5, CPB])
        rstd = sb("rstd", [P, 5, CPB])
        neg_half = sb("neg_half", [P, CPB])
        mixing = sb("mixing", [P, 7, BANK])
        mixing_xT = sb("mixing_xT", [P, BANK + 1])

        bank = [ctx.enter_context(nc.psum_tensor(f"bank{i}", [P, BANK], F32)) for i in range(8)]
        ST_BANKS, MAX_BANKS, CTX_BANK, MISC_BANK = (0, 1, 2), (3, 4, 5), 6, 7

        pe_st, pe_max, pe_ctx, pe_misc = (signal(n) for n in ("pe_st", "pe_max", "pe_ctx", "pe_misc"))
        act_exp, act_misc = signal("act_exp"), signal("act_misc")
        dve_max, dve_misc = signal("dve_max"), signal("dve_misc")
        pool_misc = signal("pool_misc")
        d_time, d_weights, d_out = signal("d_time"), signal("d_weights"), signal("d_out")
        d_x2_out = [signal(f"d_x2_out{b}") for b in range(B)]
        d_x = [signal(f"d_x{b}") for b in range(B)]
        d_spill = [signal(f"d_spill{b}") for b in range(B)]
        d_part, d_aug = [signal("d_part_q"), signal("d_part_k")], signal("d_aug")
        d_max_out = [signal(f"d_max_out{i}") for i in range(2)]
        d_max_in = [signal(f"d_max_in{i}") for i in range(2)]
        d_ctx = [signal(f"d_ctx{i}") for i in range(2)]
        d_den_in, d_rden_out, d_rden_in = signal("d_den_in"), signal("d_rden_out"), signal("d_rden_in")
        d_src, d_x2_in = signal("d_src"), signal("d_x2_in")

        bank_free = [None] * 8

        def dma(dst, src, sig, waits=()):
            return sp.add(lambda e: e.dma_start(dst, src), waits, sig, 16)

        def mm(dst, lhsT, rhs, waits=(), sig=None, start=True, stop=True):
            return pe.add(lambda e: e.matmul(dst, lhsT, rhs, start=start, stop=stop), waits, sig)

        def transpose(dst, src, waits=(), sig=None):
            return pe.add(lambda e: e.transpose(dst, src, ident[:, :]), waits, sig)

        def activate(dst, src, func, waits, bias=None, scale=None):
            kw = {}
            if bias is not None:
                kw["bias"] = bias
            if scale is not None:
                kw["scale"] = scale
            return act.add(lambda e: e.activation(dst, src, func, **kw), waits, act_misc)

        def gp(f, waits):
            return pool.add(f, [*waits, pool_misc.now()], pool_misc)

        def vec(f, waits, sig=None):
            return dve.add(f, waits, sig or dve_misc)

        C_TD, C_MIX, C_OMM, C_LNG, C_LNB = 0, 1, 4, 7, 8
        C_EW, C_ACTW, C_BQ, C_BK, C_BE = 9, 27, 33, 39, 45

        def column(dst, src, sig):
            return dma(dst, src.rearrange("(p a) -> p a", a=1), sig)

        def spread(dst, src, n):
            return dma(dst, src.rearrange("(a n) -> a n", a=1).to_broadcast([P, n]), d_weights)

        q_aug_f = q_aug[:, :, :, :].rearrange("p u h s -> p u (h s)").bitcast(F32)
        k_aug_f = k_aug[:, :, :, :].rearrange("p u h s -> p u (h s)").bitcast(F32)
        raw_w = q_aug_f[:, 0, :].rearrange("p (n d) -> p n d", d=D)
        WE_KV, W_KV, W_TIME = 0, 2 * NODES, 4 * NODES
        we_t = k_aug_f[:, 0, :].rearrange("p (n d) -> p n d", d=D)
        be_rows = we_t[0:We.shape[0], 30, :]
        be_cols = we_t[:, 24, 0:We.shape[0]]
        w_time_t = sb("w_time_t", [P, 4, D])
        mixing_sets = [mixing[:, :, :], q_aug_f[:, 1, 0:7 * BANK].rearrange("p (n s) -> p n s", n=7)]
        mixing_xTs = [mixing_xT[:, :], rden_bc[:, 0:BANK + 1]]
        x_nat = [node_ring[:, b, 1, :] for b in range(B)]

        def load_x(b):
            dma(x_nat[b].rearrange("p (k c) -> p k c", c=D), x[b].rearrange("(k p) c -> p k c", p=P), d_x[b])

        load_x(0)
        for i, w in enumerate((Wk, Wv, Wr, Wo)):
            dma(raw_w[:, W_TIME + i, :], w, d_time)
        column(col[:, C_TD:C_TD + 1], time_decay, d_time)
        for i, m in enumerate((mix_k, mix_v, mix_r)):
            column(col[:, C_MIX + i:C_MIX + i + 1], m.rearrange("a b c -> (a b c)"), d_time)
        column(col[:, C_LNG:C_LNG + 1], ln_g, d_time)
        column(col[:, C_LNB:C_LNB + 1], ln_b, d_time)
        time_in = d_time.now()
        load_x(1)
        spread(col[:, C_EW:C_EW + 3 * NODES], ew.rearrange("a b -> (a b)"), 3 * NODES)
        spread(col[:, C_ACTW:C_ACTW + NODES], act_w, NODES)
        dma(be_rows, be, d_weights)
        for c in range(NODES):
            (eq, ek_, ev), _ = node_sources(c)
            dma(w_edge_q[:, c, :], We[eq], d_weights)
            dma(raw_w[:, WE_KV + c, :], We[ek_], d_weights)
            dma(raw_w[:, WE_KV + NODES + c, :], We[ev], d_weights)
        for dst, w in ((raw_w[:, W_KV:W_KV + NODES, :], fWk), (raw_w[:, W_KV + NODES:W_KV + 2 * NODES, :], fWv),
                       (w_q[:, :, :], fWq), (w_o[:, :, :], fWo)):
            dma(dst, w.rearrange("n i o -> i n o"), d_weights)
        spread(out_g[:, :], fln_g, D)
        spread(out_b[:, :], fln_b, D)
        weights_in = d_weights.now()
        for b in range(2, B):
            load_x(b)

        neg_half_done = gp(lambda e: e.memset(neg_half[:, :], -0.5), ())
        done = gp(lambda e: e.memset(ident[:, :], 0.0), ())
        ident_done = gp(lambda e: e.affine_select(
            out=ident[:, :], in_=ident[:, :], compare_op=ALU.not_equal, fill=1.0, base=0,
            pattern=[[-1, P]], channel_multiplier=1), [done])
        ones_v_done = gp(lambda e: e.memset(v_aug[:, :, :, :, DH:VW], 1.0), ())

        td_done = activate(col[:, C_TD:C_TD + 1], col[:, C_TD:C_TD + 1], ACT.Exp, [time_in])
        omm_done = vec(lambda e: e.tensor_scalar(col[:, C_OMM:C_OMM + 3], col[:, C_MIX:C_MIX + 3], -1.0, 1.0,
                                                 ALU.mult, ALU.add), [time_in])

        banks_used = [0]

        def any_bank():
            banks_used[0] += 1
            return banks_used[0] % 8

        def misc_bank():
            return MISC_BANK

        def fill(i, waits, write, n=1):
            done = None
            for j in range(n):
                done = write(j, bank[i], [*waits, bank_free[i]] if j == 0 else (), pe_misc if j == n - 1 else None)
            return done

        def turn_four(i, srcs, waits):
            return fill(i, waits, lambda j, bk, w, s: transpose(bk[:, j * P:(j + 1) * P], srcs[j], w, s), len(srcs))

        folds = {}

        def time_weights():
            i = any_bank()
            done = turn_four(i, [raw_w[:, W_TIME + j, :] for j in range(4)], [ident_done, time_in])
            bank_free[i] = folds["time"] = activate(w_time_t[:, :, :].rearrange("p n d -> p (n d)"), bank[i][:, :], ACT.Copy, [done])

        def edge_transposes(k):
            def run():
                i = any_bank()
                done = turn_four(i, [raw_w[:, WE_KV + k + j, :] for j in range(4)], [ident_done, weights_in])
                bank_free[i] = folds["edge"] = activate(we_t[:, k:k + 4, :].rearrange("p n d -> p (n d)"), bank[i][:, :],
                                                        ACT.Copy, [done])
            return run

        def bias_columns():
            i = any_bank()
            n = We.shape[0]
            done = fill(i, [ident_done, weights_in], lambda j, bk, w, s: pe.add(lambda e: e.transpose(
                bk[:, 0:n], be_rows, ident[0:n, 0:n]), w, s))
            bank_free[i] = folds["be"] = activate(be_cols, bank[i][:, 0:n], ACT.Copy, [done])

        def fold(c):
            (eq, ek_, ev), _ = node_sources(c)
            ewq, ewk, ewv = (col[:, C_EW + 3 * c + i:C_EW + 3 * c + i + 1] for i in range(3))
            wk, wv = raw_w[:, W_KV + c, :], raw_w[:, W_KV + NODES + c, :]
            be_rep = we_t[:, 12 + c, :]

            def products():
                rep = gp(lambda e: e.tensor_copy(be_rep, be_cols[:, ev:ev + 1].to_broadcast([P, P])), [folds["be"]])
                operands = ((we_t[:, c, :], wk), (we_t[:, NODES + c, :], wv), (be_rep, wv), (wk, be_cols[:, ek_:ek_ + 1]))
                i = any_bank()
                done = fill(i, [folds["edge"], folds["be"], rep], lambda j, bk, w, s: mm(
                    bk[:, j * P:j * P + operands[j][1].shape[-1]], operands[j][0], operands[j][1], w, s), 4)
                for j, (dst, n, s) in enumerate(((w_k_fold[:, c, :], P, ewk), (w_v_fold[:, c, :], P, ewv),
                                                 (v_bias[:, c, :], P, ewv), (col[:, C_BK + c:C_BK + c + 1], 1, ewk))):
                    bank_free[i] = activate(dst, bank[i][:, j * P:j * P + n], ACT.Copy, [done], scale=s)
                folds[c] = bank_free[i]
                gp(lambda e: e.tensor_scalar(w_edge_q[:, c, :], w_edge_q[:, c, :], ewq, None, ALU.mult), [weights_in])
                gp(lambda e: e.tensor_scalar(col[:, C_BQ + c:C_BQ + c + 1], be_cols[:, eq:eq + 1], ewq, None, ALU.mult),
                         [folds["be"]])
                folds["pool"] = gp(lambda e: e.tensor_scalar(
                    w_o[:, c, :], w_o[:, c, :], col[:, C_ACTW + c:C_ACTW + c + 1], None, ALU.mult), [weights_in])
            return products

        def everything():
            return [s.now() for s in (pe_misc, act_misc, dve_misc)]

        def both(*fs):
            def run():
                for f in fs:
                    if f is not None:
                        f()
            return run

        def norm_stages(dst, src_, eps, area, state, before, free=lambda: []):
            s3, d3 = (t.rearrange("p (k c) -> p k c", c=D) for t in (src_, dst))

            def statistics():
                for k in range(CPB):
                    state["s"] = vec(lambda e, k=k: e.bn_stats(stats[:, area, k, :], s3[:, k, :]), [state[before]])

            def inverse():
                for k in range(CPB):
                    done = vec(lambda e, k=k: e.bn_aggr(meanvar[:, area, k, :], stats[:, area, k, :]), [state["s"]])
                done = vec(lambda e: e.tensor_scalar(vareps[:, area, :], meanvar[:, area, :, 1], eps, None, ALU.add), [done])
                state["r"] = gp(lambda e: e.tensor_tensor(rstd[:, area, :], vareps[:, area, :], neg_half[:, :], ALU.pow),
                                      [done, neg_half_done])

            def apply():
                waits = free()
                for k in range(CPB):
                    state["n"] = vec(lambda e, k=k: e.tensor_scalar(
                        d3[:, k, :], s3[:, k, :], meanvar[:, area, k, 0:1], rstd[:, area, k:k + 1], ALU.subtract, ALU.mult),
                        [state["r"], *waits])
            return [statistics, inverse, apply]

        node_ready = [None] * B
        FREE_AFTER = 5 + 1 + 1 + 6 + 3
        carried = {}

        def mixing_stages(b, hf, which, take_bank, set_free, shared=False):
            y, last, mixed, ek, ekv, er, num = (mixing_sets[which][:, i, :] for i in range(7))
            xT = mixing_xTs[which]
            xs = x_nat[b][:, hf * BANK:(hf + 1) * BANK]
            cols = slice(hf * BANK, (hf + 1) * BANK)
            td = col[:, C_TD:C_TD + 1].to_broadcast([P, BANK])
            st = {"x": d_x[b].now()}
            area = 2 * (b % 2) + hf
            free = everything if shared else (lambda: [])
            one, two = norm_stages(y, xs, LN_EPS, area, st, "x", free), norm_stages(y, y, LN_EPS, area, st, "n")
            stages = [*one[:2], both(one[2], two[0]), *two[1:]]

            def turn():
                st["i"] = i = take_bank()
                st["t"] = turn_four(i, [y[:, j * P:(j + 1) * P] for j in range(CPB)], [st["n"], ident_done])

            def turned():
                i = st["i"]
                if hf == 0:
                    pad = vec(lambda e: e.memset(xT[:, 0:1], 0.0), [set_free, *free()])
                else:
                    prev_xT, prev_done = carried[b, "xT"]
                    pad = vec(lambda e: e.tensor_copy(xT[:, 0:1], prev_xT[:, BANK:BANK + 1]), [prev_done, set_free, *free()])
                bank_free[i] = st["xT"] = activate(xT[:, 1:BANK + 1], bank[i][:, :], ACT.Identity, [st["t"], pad, set_free, *free()],
                                                   bias=col[:, C_LNB:C_LNB + 1], scale=col[:, C_LNG:C_LNG + 1])
                carried[b, "xT"] = (xT, st["xT"])
            stages.append((turn, turned))
            parts_of = []
            for n in range(3):
                mix, omm = (col[:, cc + n:cc + n + 1] for cc in (C_MIX, C_OMM))

                def older(omm=omm):
                    st["a"] = gp(lambda e: e.tensor_scalar(last, xT[:, 0:BANK], omm, None, ALU.mult),
                                       [st["xT"], omm_done, st.get("m"), set_free, *free()])

                def mixes(mix=mix):
                    st["m"] = vec(lambda e: e.scalar_tensor_tensor(
                        out=mixed, in0=xT[:, 1:BANK + 1], scalar=mix, in1=last, op0=ALU.mult, op1=ALU.add),
                        [st["a"], st.get("p"), set_free, *free()])

                def project(n=n):
                    st["i"] = i = take_bank()
                    st["p"] = fill(i, [st["m"], folds["time"]], lambda j, bk, w, s: mm(bk[:, :], w_time_t[:, n, :], mixed, w, s))

                def projected(n=n):
                    i = st["i"]
                    if n == 0:
                        bank_free[i] = st["k"] = activate(ek, bank[i][:, :], ACT.Exp, [st["p"], set_free, *free()])
                    elif n == 1:
                        bank_free[i] = st["v"] = vec(lambda e: e.tensor_tensor(ekv, bank[i][:, :], ek, ALU.mult),
                                                             [st["p"], st["k"], *free()])
                    else:
                        bank_free[i] = st["r0"] = activate(er, bank[i][:, :], ACT.Exp, [st["p"], set_free, *free()],
                                                              scale=-1.0)
                parts_of.append((older, mixes, (project, projected)))
            stages.append(parts_of[0][0])
            for n in range(3):
                stages += [both(parts_of[n][1], parts_of[n + 1][0] if n < 2 else None), parts_of[n][2]]
            den = y

            def scan(dst, data, key):
                def run():
                    start, before = (0.0, None) if hf == 0 else carried[b, key]
                    st[key] = vec(lambda e: e.tensor_tensor_scan(dst, td, data, start, ALU.mult, ALU.add),
                                  [td_done, st["k"], st["v"], before, *free()])
                    keep = carried_col[:, b % 2, ("den", "num").index(key):("den", "num").index(key) + 1]
                    if hf == 0:
                        carried[b, key] = (keep, vec(lambda e: e.tensor_copy(keep, dst[:, BANK - 1:BANK]), [st[key]]))
                return run

            def one_more():
                st["r1"] = gp(lambda e: e.tensor_scalar(er, er, 1.0, None, ALU.add), [st["r0"]])

            def product():
                st["q"] = vec(lambda e: e.scalar_tensor_tensor(out=er, in0=den, scalar=WKV_EPS, in1=er, op0=ALU.add, op1=ALU.mult),
                              [st["den"], st["r1"]])

            def invert(k):
                def run():
                    st["inv"] = vec(lambda e: e.reciprocal(ek[:, k * P:(k + 1) * P], er[:, k * P:(k + 1) * P]), [st["q"], st["den"]])
                return run

            def gate():
                st["g"] = gp(lambda e: e.tensor_tensor(ekv, num, ek, ALU.mult), [st["inv"], st["num"]])

            def out_project():
                st["i"] = i = take_bank()
                st["o"] = fill(i, [st["g"]], lambda j, bk, w, s: mm(
                    bk[:, j * P:(j + 1) * P], ekv[:, j * P:(j + 1) * P], w_time_t[:, 3, :], w, s), CPB)

            def residual():
                i = st["i"]
                bank_free[i] = st["x2"] = vec(lambda e: e.tensor_tensor(xs, bank[i][:, :], xs, ALU.add), [st["o"]])

            def store_x2():
                dma(x2_dram[b, :, hf * CPB:(hf + 1) * CPB, :], xs.rearrange("p (k c) -> p k c", c=D), d_x2_out[b], [st["x2"]])

            stages += [both(one_more, scan(den, ek, "den")), scan(num, ekv, "num"), product]
            assert len(stages) == FREE_AFTER
            stages += [both(invert(k), invert(k + 1)) for k in range(0, CPB, 2)] + [gate, (out_project, residual)]
            last_norm = norm_stages(num, xs, LN_EPS, area, st, "x2", free)
            stages += [both(store_x2, last_norm[0]), *last_norm[1:]]

            def turn_out():
                st["i"] = i = take_bank()
                st["t"] = turn_four(i, [num[:, j * P:(j + 1) * P] for j in range(CPB)], [st["n"]])

            def turned_out():
                i = st["i"]
                bank_free[i] = node_ready[b] = activate(node_ring[:, b, 0, cols], bank[i][:, :], ACT.Copy, [st["t"]])
                carried[b, "end", hf] = node_ready[b]
                if hf == NHALF - 1:
                    dma(node_dram[0, b], node_ring[:, b, 0, :], d_spill[b], [node_ready[b], carried[b, "end", 0]])
            stages.append((turn_out, turned_out))
            return stages

        def run_stage(stage):
            for f in (stage if isinstance(stage, tuple) else (stage,)):
                f()

        def run_side_by_side(lists):
            for t in range(max(o + len(l) for o, l in lists)):
                for o, l in lists:
                    if 0 <= t - o < len(l):
                        run_stage(l[t - o])

        first = [mixing_stages(0, hf, hf, any_bank, None) for hf in range(NHALF)]
        weight_stages = [edge_transposes(k) for k in range(0, 2 * NODES, 4)] + [bias_columns] + [fold(c) for c in range(NODES)]
        run_side_by_side([(0, [time_weights]), (0, first[0]), (3, first[1]), (6, weight_stages)])
        weights_done = [pe_misc.now(), act_misc.now(), folds["pool"]]

        ones_k_done = [None, None]

        def ones_k(u):
            def run():
                ones_k_done[u] = gp(lambda e: e.memset(
                    k_aug[SPLIT_ROWS:AUG_ROWS, u, :, :].rearrange("p h s -> p (h s)"), 1.0), weights_done)
            return run
        ones_k(0)()
        ones_k(1)()

        counts = dict(st=0, mx=0, e=0)
        e_free = [None] * E_SLOTS
        aug_in, part_out = {}, {}
        max_rows_in = {}
        v_ready, v_read = {}, {}
        ctx_moved = {}
        last_st = {}

        def misc_fill(waits, write, n=1):
            return fill(MISC_BANK, waits, write, n)

        src_read = [None]

        def load_source(u, which):
            c, b = divmod(u, B)
            if c > 0:
                dma(src[:, :], node_dram[node_sources(c)[1][which] + 1, b], d_src, [d_spill[b].now(), src_read[0]])

        def source(u, cols):
            c, b = divmod(u, B)
            return (node_ring[:, b, 0, cols], node_ready[b]) if c == 0 else (src[:, cols], d_src.now())

        def project_q(u, hf):
            c, b = divmod(u, B)
            cols = slice(hf * BANK, (hf + 1) * BANK)
            done = misc_fill([node_ready[b], *weights_done], lambda j, bk, w, s: mm(
                bk[:, :], w_edge_q[:, c, :], node_ring[:, b, c % 2, cols], w, s))
            bank_free[MISC_BANK] = activate(node_ring[:, b, (c + 1) % 2, cols], bank[MISC_BANK][:, :], ACT.Identity,
                                            [done, d_spill[b].now(), d_x2_out[b].now()], bias=col[:, C_BQ + c:C_BQ + c + 1])
            return bank_free[MISC_BANK]

        q_done = {}
        split_done = {}

        def project_head(u, side, hf):
            c, b = divmod(u, B)
            cols = slice(hf * BANK, (hf + 1) * BANK)
            w_ = (w_q, w_k_fold)[side]
            data, ready = (node_ring[:, b, (c + 1) % 2, cols], q_done.get((u, hf))) if side == 0 else source(u, cols)
            done = misc_fill([ready, *weights_done], lambda j, bk, w, s: mm(bk[:, :], w_[:, c, :], data, w, s))
            if side == 1:
                src_read[0] = done
            p1 = part[side][:, 0, cols]
            bias = col[:, C_BK + c:C_BK + c + 1]
            if side == 0:
                p1_done = activate(p1, bank[MISC_BANK][:, :], ACT.Copy, [done, d_part[side].now()])
            else:
                p1_done = activate(p1, bank[MISC_BANK][:, :], ACT.Identity, [done, d_part[side].now()], bias=bias)
            split_done[u, side, hf, 1] = p1_done

        def split_rest(u, side, hf):
            c, _ = divmod(u, B)
            cols = slice(hf * BANK, (hf + 1) * BANK)
            p1, r = part[side][:, 0, cols], rest[:, cols]
            bias = 0.0 if side == 0 else col[:, C_BK + c:C_BK + c + 1]
            waits = [split_done[u, side, hf, 1], split_done.get((u, 1) if side == 0 else (u - 1, 0))]
            if side == 0:
                bank_free[MISC_BANK] = vec(lambda e: e.tensor_tensor(r, bank[MISC_BANK][:, :], p1, ALU.subtract), waits)
            else:
                bank_free[MISC_BANK] = vec(lambda e: e.scalar_tensor_tensor(
                    out=r, in0=bank[MISC_BANK][:, :], scalar=bias, in1=p1, op0=ALU.add, op1=ALU.subtract), waits)
            split_done[u, side, hf, 2] = bank_free[MISC_BANK]

        def split_low(u, side, hf):
            cols = slice(hf * BANK, (hf + 1) * BANK)
            r, p2, p3 = rest[:, cols], part[side][:, 1, cols], part[side][:, 2, cols]
            done = act.add(lambda e: e.activation(p2, r, ACT.Copy), [split_done[u, side, hf, 2]], act_misc)
            split_done[u, side] = gp(lambda e: e.tensor_tensor(p3, r, p2, ALU.subtract), [done])

        def store_parts(u, side):
            waits = [split_done[u, side]]
            for p in range(3):
                part_out[u, side] = dma(part_dram[u % 2, side, p], part[side][:, p, :], d_part[side], waits)

        def load_aug(u):
            waits = [part_out[u, 0], part_out[u, 1], last_st.get(u - 2), *weights_done]
            for side, (aug, slots) in enumerate(((q_aug, Q_SLOTS), (k_aug, K_SLOTS))):
                for i, p in enumerate(slots):
                    aug_in[u] = dma(aug[i * DH:(i + 1) * DH, u % 2, :, :],
                                    part_dram[u % 2, side, p].rearrange("(h d) s -> d h s", d=DH), d_aug, waits)

        def project_v(u, hf):
            c, _ = divmod(u, B)
            k0 = hf * CPB
            data, ready = source(u, slice(k0 * P, (k0 + CPB) * P))
            done = src_read[0] = misc_fill([ready, *weights_done], lambda j, bk, w, s: mm(
                bk[:, j * P:(j + 1) * P], data[:, j * P:(j + 1) * P], w_v_fold[:, c, :], w, s), CPB)
            bias = v_bias[:, c, :].rearrange("p (o h d) -> p o h d", o=1, h=H).to_broadcast([P, CPB, H, DH])
            bank_free[MISC_BANK] = v_ready[u] = vec(lambda e: e.tensor_tensor(
                v_aug[:, u % 2, k0:k0 + CPB, :, 0:DH],
                bank[MISC_BANK][:, :].rearrange("p (k h d) -> p k h d", k=CPB, h=H), bias, ALU.add),
                [done, v_read.get(u - 2), ones_v_done])

        def max_rows(G):
            u, g = divmod(G, GPU)
            hg, qh = divmod(g, NHALF)
            r = G % 2
            NR = HG * CPB
            state = {}

            def combine():
                state["col"] = combined[G] = vec(lambda e: e.tensor_reduce(max_col[:, r, :], max_half[:, r, :, :], AX_X, ALU.max),
                                                 [dve_max.now()])

            def turn():
                i = state["i"] = MAX_BANKS[counts["mx"] % len(MAX_BANKS)]
                counts["mx"] += 1
                state["t"] = pe.add(lambda e: e.transpose(bank[i][0:NR, 0:P], max_col[:, r, :], ident[:, :]),
                                    [state["col"], bank_free[i]], pe_max)

            def negate():
                i = state["i"]
                state["m"] = bank_free[i] = vec(lambda e: e.tensor_scalar(
                    max_neg[:, r, :], bank[i][0:NR, 0:P], -1.0, None, ALU.mult), [state["t"], splits.get(G - 2)])

            def split():
                p = [max_part[:, r, i, :] for i in range(3)]
                neg, left = max_neg[:, r, :], max_rest[:, r, :]
                a = activate(p[0], neg, ACT.Copy, [state["m"], d_max_out[r].now()])
                b_ = gp(lambda e: e.tensor_tensor(left, neg, p[0], ALU.subtract), [a])
                state["rest"] = b_

            def split2():
                p = [max_part[:, r, i, :] for i in range(3)]
                left = max_rest[:, r, :]
                c_ = activate(p[1], left, ACT.Copy, [state["rest"]])
                splits[G] = state["s"] = gp(lambda e: e.tensor_tensor(p[2], left, p[1], ALU.subtract), [c_])

            def move():
                o = dma(max_dram[r].rearrange("i n s -> n i s"), max_part[:, r, :, :], d_max_out[r], [state["s"]])
                max_rows_in[G] = dma(
                    q_aug[SPLIT_ROWS:AUG_ROWS, u % 2, hg * HG:(hg + 1) * HG, qh * BANK:(qh + 1) * BANK],
                    max_dram[r].rearrange("i (h t) s -> i h (t s)", h=HG), d_max_in[r], [o, last_st.get(u - 2)])
            combine()
            return {0: [None, both(turn, negate)], 1: [split, split2], 2: [move, None]}

        splits = {}

        def evacuate_ctx(G, pv_done):
            u, g = divmod(G, GPU)
            hg, qh = divmod(g, NHALF)
            r = G % 2
            bank_free[CTX_BANK] = done = activate(raw[:, r, :], bank[CTX_BANK][:, :], ACT.Copy, [pv_done, d_ctx[r].now()])

            def move():
                cols = slice(qh * BANK, (qh + 1) * BANK)
                for j in range(HG):
                    h = hg * HG + j
                    dma(ctxT[h * DH:(h + 1) * DH, cols], raw[j * VW:j * VW + DH, r, :], d_ctx[r], [done, out_read.get(u - 1)])
                ctx_moved[G] = dma(den_dram[u % 2, hg * HG:(hg + 1) * HG, cols], raw[DH:P:VW, r, :], d_ctx[r], [done])
            return move

        out_read = {}

        def finish_unit(u):
            c, b = divmod(u, B)
            state = {}

            def load_den():
                dma(den_pack[:, :], den_dram[u % 2].rearrange("h (a s) -> (h a) s", s=H * S // P), d_den_in,
                    [ctx_moved[u * GPU + g] for g in range(GPU)])

            def reciprocal():
                state["r"] = vec(lambda e: e.reciprocal(rden_pack[:, :], den_pack[:, :]), [d_den_in.now(), d_rden_out.now()])

            def spread_rden():
                o = dma(rden_dram[u % 2].rearrange("h (a s) -> (h a) s", s=H * S // P), rden_pack[:, :], d_rden_out, [state["r"]])
                for h in range(H):
                    dma(rden_bc[h * DH:(h + 1) * DH, :], rden_dram[u % 2, h:h + 1, :].to_broadcast([DH, S]), d_rden_in,
                        [o, pool_misc.now(), dve_misc.now()])

            def normalise():
                state["n"] = gp(lambda e: e.tensor_tensor(ctxT[:, :], ctxT[:, :], rden_bc[:, :], ALU.mult),
                                      [d_rden_in.now(), ctx_moved[u * GPU + GPU - 1], ctx_moved[u * GPU + GPU - 2]])

            def project(hf):
                def run():
                    cols = slice(hf * BANK, (hf + 1) * BANK)
                    node = node_ring[:, b, (c + 1) % 2, cols]
                    done = misc_fill([state["n"]], lambda j, bk, w, s: mm(bk[:, :], w_o[:, c, :], ctxT[:, cols], w, s))
                    bank_free[MISC_BANK] = node_ready[b] = vec(lambda e: e.tensor_tensor(node, bank[MISC_BANK][:, :], node, ALU.add), [done])
                    out_read[u] = done
                return run

            def spill():
                if c < SPILLED:
                    dma(node_dram[c + 1, b], node_ring[:, b, (c + 1) % 2, :], d_spill[b], [node_ready[b]])
            stages = {3: [load_den], 5: [reciprocal], 6: [spread_rden], 11: [normalise], 13: [project(0)], 14: [project(1)]}
            stages.update(finish_batch(u) if c == NODES - 1 else {15: [spill]})
            return stages

        def finish_batch(u):
            c, b = divmod(u, B)
            y, x2 = rden_bc, src
            yb = y[:, :]
            state = {}

            def turn(hf):
                def run():
                    k0 = hf * CPB
                    done = misc_fill([node_ready[b]], lambda j, bk, w, s: transpose(
                        bk[:, j * P:(j + 1) * P], node_ring[:, b, (c + 1) % 2, (k0 + j) * P:(k0 + j + 1) * P], w, s), CPB)
                    bank_free[MISC_BANK] = state["y"] = activate(y[:, k0 * P:(k0 + CPB) * P], bank[MISC_BANK][:, :], ACT.Copy, [done])
                    if hf == 0:
                        dma(x2[:, :].rearrange("p (k c) -> p k c", c=D), x2_dram[b], d_x2_in, [src_read[0], d_x2_out[b].now()])
                return run

            halves = [norm_stages(yb[:, hf * BANK:(hf + 1) * BANK], yb[:, hf * BANK:(hf + 1) * BANK], LN_EPS_OUT, 4, state, "y")
                      for hf in range(NHALF)]

            def affine():
                y3 = yb.rearrange("p (k c) -> p k c", c=D)
                g3, b3 = (t[:, :].rearrange("p (o c) -> p o c", o=1).to_broadcast([P, NCH, D]) for t in (out_g, out_b))
                a = gp(lambda e: e.tensor_tensor(y3, y3, g3, ALU.mult), [state["n"]])
                a = gp(lambda e: e.tensor_tensor(y3, y3, b3, ALU.add), [a])
                state["o"] = src_read[0] = gp(lambda e: e.tensor_tensor(yb, yb, x2[:, :], ALU.add), [a, d_x2_in.now()])

            def store():
                dma(out[b].rearrange("(k p) c -> p k c", p=P), yb.rearrange("p (k c) -> p k c", c=D), d_out, [state["o"]])
            return {15: [turn(0)], 16: [turn(1)], 17: halves[0][:2], 18: [halves[0][2], halves[1][0]], 19: halves[1][1:],
                    20: [affine], 22: [store]}

        def projection_stages(u):
            def q(hf):
                def run():
                    q_done[u, hf] = project_q(u, hf)
                return run
            return {0: [q(0)], 1: [q(1)],
                    2: [lambda: project_head(u, 1, 0), lambda: split_rest(u, 1, 0)],
                    3: [lambda: project_head(u, 1, 1), lambda: split_rest(u, 1, 1)],
                    4: [lambda: split_low(u, 1, 0), lambda: split_low(u, 1, 1)],
                    5: [lambda: project_head(u, 0, 0), lambda: split_rest(u, 0, 0)],
                    6: [lambda: (store_parts(u, 1), project_head(u, 0, 1)), lambda: split_rest(u, 0, 1)],
                    7: [lambda: split_low(u, 0, 0), lambda: split_low(u, 0, 1)], 8: [lambda: store_parts(u, 0)], 9: [lambda: load_aug(u)]}

        def score_tile(G, chunk, j):
            u, g = divmod(G, GPU)
            hg, qh = divmod(g, NHALF)
            h = hg * HG + j
            n = counts["st"]
            counts["st"] += 1
            i = ST_BANKS[n % len(ST_BANKS)]
            last_st[u] = done = mm(bank[i][:, :], k_aug[0:AUG_ROWS, u % 2, h, chunk * P:(chunk + 1) * P],
                                   q_aug[0:AUG_ROWS, u % 2, h, qh * BANK:(qh + 1) * BANK],
                                   [bank_free[i], max_rows_in[G], aug_in[u], ones_k_done[u % 2]], pe_st)
            bank_free[i] = act.add(lambda e: e.activation(e_ring[:, n % E_SLOTS, :], bank[i][:, :], ACT.Exp, scale=EXP_SCALE),
                                 [done, e_free[n % E_SLOTS]], act_exp)
            return n % E_SLOTS, bank_free[i]

        def max_tile(G, t):
            u, g = divmod(G, GPU)
            hg, qh = divmod(g, NHALF)
            row, kh = divmod(t, NHALF)
            j, qt = divmod(row, CPB)
            h = hg * HG + j
            q0 = qh * BANK + qt * P
            i = MAX_BANKS[counts["mx"] % len(MAX_BANKS)]
            counts["mx"] += 1
            done = mm(bank[i][:, :], q_aug[0:SPLIT_ROWS, u % 2, h, q0:q0 + P],
                      k_aug[0:SPLIT_ROWS, u % 2, h, kh * BANK:(kh + 1) * BANK], [bank_free[i], aug_in[u]], pe_max)
            bank_free[i] = dve.add(lambda e: e.tensor_reduce(max_half[:, G % 2, row, kh:kh + 1], bank[i][:, :],
                                                            AX_X, ALU.max), [done, combined.get(G - 2)], dve_max)

        combined = {}

        def context(G, chunk, tiles):
            u, g = divmod(G, GPU)
            hg = g // NHALF
            for j, (slot, ready) in enumerate(tiles):
                done = mm(bank[CTX_BANK][j * VW:(j + 1) * VW, :], v_aug[:, u % 2, chunk, hg * HG + j, :], e_ring[:, slot, :],
                          [ready, v_ready[u], bank_free[CTX_BANK] if chunk == 0 else None], pe_ctx if j == HG - 1 else None,
                          start=(chunk == 0), stop=(chunk == NCH - 1))
            for slot, _ in tiles:
                e_free[slot] = done
            v_read[u] = done
            return done

        due = {}

        def schedule(at, stages):
            for chunk, halves in stages.items():
                for k, stage in enumerate(halves):
                    if stage is None:
                        continue
                    due.setdefault(2 * (at + chunk) + k, []).append(stage)

        UNIT_CHUNKS = GPU * NCH
        MAX_TILES = HG * CPB * NHALF // NCH

        taken = set()

        def reserve(at, stages, fills):
            schedule(at, stages)
            assert not taken & {at + k for k in fills}
            taken.update(at + k for k in fills)

        def place(at, stages):
            half = 2 * at
            for stage in stages:
                if isinstance(stage, tuple):
                    half += half % 2
                    while half // 2 in taken:
                        half += 2
                    taken.add(half // 2)
                    schedule(half // 2, {0: list(stage)})
                    half += 2
                else:
                    due.setdefault(half, []).append(stage)
                    half += 1
            return -(-half // 2)

        PROJECT_AT = [None, 5, 6, 6] + [1] * (UNITS - 4)
        for u in range(UNITS):
            if u > 0:
                slot = (u - 1) * UNIT_CHUNKS
                at = PROJECT_AT[u]
                schedule(slot, {0: [lambda u=u: load_source(u, 0)], 23: [lambda u=u: load_source(u, 1)]})
                reserve(slot, {25: [lambda u=u: project_v(u, 0)], 26: [lambda u=u: project_v(u, 1)]}, (25, 26))
                reserve(slot + at, projection_stages(u), (0, 1, 2, 3, 5, 6))
            reserve((u + 1) * UNIT_CHUNKS, finish_unit(u), (13, 14) + ((15, 16) if u // B == NODES - 1 else ()))

        second = [mixing_stages(1, hf, hf, lambda: bank_choice[0](), pe_misc.now()) for hf in range(NHALF)]
        bank_choice = [any_bank]
        unit0 = [s for halves in projection_stages(0).values() for s in halves]
        unit0 += [lambda: project_v(0, 0), lambda: project_v(0, 1)]
        AHEAD = 6
        run_side_by_side([(0, unit0), (0, second[0][:AHEAD]), (2, second[1][:AHEAD])])
        bank_choice[0] = misc_bank
        start = -LOOKAHEAD * NCH
        middle = place(start, second[0][AHEAD:FREE_AFTER])
        ends = [place(middle, second[0][FREE_AFTER:]), place(start + 1, second[1][AHEAD:])]
        assert max(ends) <= PROJECT_AT[1], ends
        at = middle + 2
        for b in range(2, B):
            for hf in range(NHALF):
                half = mixing_stages(b, hf, 0, misc_bank, None, shared=True)
                middle = place(at, half[:FREE_AFTER])
                end = place(middle, half[FREE_AFTER:])
                at = middle + 1
            assert end <= (b - 1) * UNIT_CHUNKS + PROJECT_AT[b], (b, end)

        previous = None
        last_step = (UNITS + 1) * UNIT_CHUNKS
        for step in range(-LOOKAHEAD * NCH, last_step):
            G, chunk = divmod(step, NCH)
            tiles = []
            for j in range(HG):
                if 0 <= G < GROUPS:
                    tiles.append(score_tile(G, chunk, j))
                if G + LOOKAHEAD < GROUPS:
                    max_tile(G + LOOKAHEAD, chunk * MAX_TILES + j)
                if j % 2:
                    for stage in due.pop(2 * step + j // 2, ()):
                        stage()
            if previous is not None:
                done = context(*previous)
                if previous[1] == NCH - 1:
                    wait = 6 if previous[0] % GPU == 0 else 0
                    schedule(step + 1, {wait: [evacuate_ctx(previous[0], done)]})
            previous = (G, chunk, tiles) if tiles else None
            if chunk == NCH - 1 and G + LOOKAHEAD < GROUPS:
                schedule(step + 1, max_rows(G + LOOKAHEAD))
        assert not due, sorted(due)

        sp.add(None, [s.now() for s in signals if s.count])

        with nc.Block() as block:
            @block.tensor
            def _(e):
                pe.play(e)

            @block.scalar
            def _(e):
                act.play(e)

            @block.vector
            def _(e):
                dve.play(e)

            @block.gpsimd
            def _(e):
                pool.play(e)

            @block.sync
            def _(e):
                sp.play(e)


_INS = ["L0_attn_x", "L0_attn_time_decay", "L0_attn_time_mix_k", "L0_attn_time_mix_v", "L0_attn_time_mix_r",
        "L0_attn_Wk", "L0_attn_Wv", "L0_attn_Wr", "L0_attn_Wo", "L0_attn_ln_g", "L0_attn_ln_b", "L0_ffn_ew",
        "L0_ffn_act_w", "L0_ffn_We", "L0_ffn_be", "L0_ffn_Wq", "L0_ffn_Wk", "L0_ffn_Wv", "L0_ffn_Wo",
        "L0_ffn_ln_g", "L0_ffn_ln_b"]


def kernel(**inputs):
    import numpy as _np
    import concourse.bacc as _bacc
    from concourse import mybir as _mybir
    from concourse.bass_utils import run_bass_kernel_spmd as _run

    nc = _bacc.Bacc("TRN2", target_bir_lowering=False, num_devices=1)
    arrays, args = {}, []
    for name in _INS:
        a = _np.ascontiguousarray(inputs[name])
        arrays[f"in_{name}"] = a
        args.append(nc.dram_tensor(f"in_{name}", a.shape, _mybir.dt.from_np(a.dtype), kind="ExternalInput").ap())
    out = nc.dram_tensor("out_0", arrays["in_L0_attn_x"].shape, F32, kind="ExternalOutput").ap()
    build(nc, *args, out)
    r = _run(nc, [arrays], core_ids=[0])
    return r.results[0]["out_0"]
```

```python
from contextlib import ExitStack

import concourse.bass as bass
from concourse import mybir

F32 = mybir.dt.float32
BF16 = mybir.dt.bfloat16
ALU = mybir.AluOpType
ACT = mybir.ActivationFunctionType
AX_X = mybir.AxisListType.X

P = 128
BANK = 512
NODES = 6
MAX_PREV = 5
H = 8
VW = 32
HG = P // VW
SECOND_HALF, WEIGHTS, SECOND_BATCH, THIRD_BATCH = 2, 8, 6, 10
LOOKAHEAD = 14
E_SLOTS = 10
Q_SLOTS = (0, 1, 2, 0, 1, 0)
K_SLOTS = (0, 1, 0, 1, 0, 2)
LN_EPS = 1e-5
LN_EPS_OUT = 1e-6
WKV_EPS = 1e-8


class Signal:

    def __init__(self, handle):
        self.handle = handle
        self.count = 0

    def now(self):
        return (self, self.count)


class Queue:

    def __init__(self):
        self.steps = []

    def add(self, issue, waits=(), signal=None, by=1):
        if signal is not None:
            signal.count += by
        self.steps.append((issue, [w for w in waits if w is not None], signal, by))
        return None if signal is None else signal.now()

    def play(self, engine):
        reached = {}
        for issue, waits, signal, by in self.steps:
            for sig, value in waits:
                if reached.get(sig, 0) < value:
                    engine.wait_ge(sig.handle, value)
                    reached[sig] = value
            instruction = issue(engine) if issue is not None else None
            if signal is not None:
                instruction.then_inc(signal.handle, by)


def ascending_runs(slots):
    runs = []
    for i, part in enumerate(slots):
        if runs and part == runs[-1][1] + runs[-1][2]:
            runs[-1][2] += 1
        else:
            runs.append([i, part, 1])
    return runs


def node_sources(c):
    first = sum(min(i + 1, MAX_PREV) for i in range(c))
    n = min(c + 1, MAX_PREV)
    return (first + n - 1, first, first + n // 2), (c - n, c - n + n // 2)


def build(nc, x, time_decay, mix_k, mix_v, mix_r, Wk, Wv, Wr, Wo, ln_g, ln_b, ew, act_w, We, be,
          fWq, fWk, fWv, fWo, fln_g, fln_b, out):
    B, S, D = x.shape
    DH = D // H
    NCH = S // P
    NHALF = S // BANK
    CPB = BANK // P
    assert B == 4 and D == P and DH * len(Q_SLOTS) + 3 <= P and H % HG == 0
    UNITS = NODES * B
    GPU = (H // HG) * NHALF
    GROUPS = UNITS * GPU
    SPLIT_ROWS = DH * len(Q_SLOTS)
    AUG_ROWS = SPLIT_ROWS + 3
    EXP_SCALE = DH ** -0.5
    SPILLED = NODES - 3

    pe, act, dve, pool, sp = Queue(), Queue(), Queue(), Queue(), Queue()
    ctx = ExitStack()
    with ctx:
        def sb(name, shape, dt=F32):
            return ctx.enter_context(nc.sbuf_tensor(name, shape, dt))

        signals = []

        def signal(name):
            s = Signal(ctx.enter_context(nc.semaphore(name)))
            signals.append(s)
            return s

        def dram(name, shape, dt=F32):
            return nc.dram_tensor(name, shape, dt, kind="Internal").ap()

        x2_dram = dram("x2_dram", [B, P, NCH, D])
        node_dram = dram("node_dram", [SPILLED + 1, B, P, S])
        part_dram = dram("part_dram", [2, 2, 3, P, S], BF16)
        max_dram = dram("max_dram", [2, 3, HG * CPB, P], BF16)
        den_dram = dram("den_dram", [2, H, S])
        rden_dram = dram("rden_dram", [2, H, S])

        node_ring = sb("node_ring", [P, B, 2, S])
        q_aug = sb("q_aug", [P, 2, H, S], BF16)
        k_aug = sb("k_aug", [P, 2, H, S], BF16)
        e_ring = sb("e_ring", [P, E_SLOTS, BANK])
        v_aug = sb("v_aug", [P, 2, NCH, H, VW])
        src = sb("src", [P, S])
        part = [sb("q_part", [P, 3, S], BF16), sb("k_part", [P, 3, S], BF16)]
        rest = sb("rest", [P, S])
        raw = sb("raw", [P, 2, BANK])
        ctxT = sb("ctxT", [P, S])
        rden_bc = sb("rden_bc", [P, S])
        den_pack = sb("den_pack", [P, H * S // P])
        rden_pack = sb("rden_pack", [P, H * S // P])
        w_edge_q = sb("w_edge_q", [P, NODES, D])
        w_q = sb("w_q", [P, NODES, D])
        w_o = sb("w_o", [P, NODES, D])
        w_k_fold = sb("w_k_fold", [P, NODES, D])
        w_v_fold = sb("w_v_fold", [P, NODES, D])
        v_bias = sb("v_bias", [P, NODES, D])
        col = sb("col", [P, 64])
        ident = sb("ident", [P, P])
        carried_col = sb("carried_col", [P, B, 2])
        out_g = sb("out_g", [P, D])
        out_b = sb("out_b", [P, D])
        max_half = sb("max_half", [P, 2, HG * CPB, 2])
        max_col = sb("max_col", [P, 2, HG * CPB])
        max_neg = sb("max_neg", [HG * CPB, 2, P])
        max_rest = sb("max_rest", [HG * CPB, 2, P])
        max_part = sb("max_part", [HG * CPB, 2, 3, P], BF16)
        stats = sb("stats", [P, 2 * B + 1, CPB, 6])
        meanvar = sb("meanvar", [P, 2 * B + 1, CPB, 2])
        vareps = sb("vareps", [P, 2 * B + 1, CPB])
        rstd = sb("rstd", [P, 2 * B + 1, CPB])
        neg_half = sb("neg_half", [P, CPB])
        mixing = sb("mixing", [P, 6, BANK])
        mixing_xT = sb("mixing_xT", [P, BANK + 1])

        bank = [ctx.enter_context(nc.psum_tensor(f"bank{i}", [P, BANK], F32)) for i in range(8)]
        ST_BANKS, MAX_BANKS, CTX_BANK, MISC_BANK = (0, 1, 2), (3, 4, 5), 6, 7

        pe_st, pe_max, pe_ctx, pe_misc = (signal(n) for n in ("pe_st", "pe_max", "pe_ctx", "pe_misc"))
        act_exp, act_misc = signal("act_exp"), signal("act_misc")
        dve_max, dve_misc = signal("dve_max"), signal("dve_misc")
        pool_misc = signal("pool_misc")
        d_time, d_weights, d_out = signal("d_time"), signal("d_weights"), signal("d_out")
        d_x2_out = [signal(f"d_x2_out{b}") for b in range(B)]
        d_x = [signal(f"d_x{b}") for b in range(B)]
        d_spill = [signal(f"d_spill{b}") for b in range(B)]
        d_part, d_aug = [signal("d_part_q"), signal("d_part_k")], [signal(f"d_aug{i}") for i in range(H // HG)]
        d_max_out = [signal(f"d_max_out{i}") for i in range(2)]
        d_max_in = [signal(f"d_max_in{i}") for i in range(2)]
        d_ctx = [signal(f"d_ctx{i}") for i in range(2)]
        d_den_in, d_rden_out, d_rden_in = signal("d_den_in"), signal("d_rden_out"), signal("d_rden_in")
        d_last_den = signal("d_last_den")
        d_x2_last = [signal(f"d_x2_last{i}") for i in range(NHALF)]
        d_src, d_x2_in = signal("d_src"), signal("d_x2_in")

        bank_free = [None] * 8

        def dma(dst, src, sig, waits=()):
            return sp.add(lambda e: e.dma_start(dst, src), waits, sig, 16)

        def mm(dst, lhsT, rhs, waits=(), sig=None, start=True, stop=True):
            return pe.add(lambda e: e.matmul(dst, lhsT, rhs, start=start, stop=stop), waits, sig)

        def transpose(dst, src, waits=(), sig=None):
            return pe.add(lambda e: e.transpose(dst, src, ident[:, :]), waits, sig)

        def activate(dst, src, func, waits, bias=None, scale=None):
            kw = {}
            if bias is not None:
                kw["bias"] = bias
            if scale is not None:
                kw["scale"] = scale
            return act.add(lambda e: e.activation(dst, src, func, **kw), waits, act_misc)

        def gp(f, waits):
            return pool.add(f, [*waits, pool_misc.now()], pool_misc)

        def vec(f, waits, sig=None):
            return dve.add(f, waits, sig or dve_misc)

        C_TD, C_MIX, C_OMM, C_LNG, C_LNB = 0, 1, 4, 7, 8
        C_EW, C_ACTW, C_BQ, C_BK, C_BE = 9, 27, 33, 39, 45

        def column(dst, src, sig):
            return dma(dst, src.rearrange("(p a) -> p a", a=1), sig)

        def spread(dst, src, n):
            return dma(dst, src.rearrange("(a n) -> a n", a=1).to_broadcast([P, n]), d_weights)

        q_aug_f = q_aug[:, :, :, :].rearrange("p u h s -> p u (h s)").bitcast(F32)
        k_aug_f = k_aug[:, :, :, :].rearrange("p u h s -> p u (h s)").bitcast(F32)
        raw_w = q_aug_f[:, 0, :].rearrange("p (n d) -> p n d", d=D)
        WE_KV, W_KV, W_TIME = 0, 2 * NODES, 4 * NODES
        we_t = k_aug_f[:, 0, :].rearrange("p (n d) -> p n d", d=D)
        be_rows = we_t[0:We.shape[0], 30, :]
        be_cols = we_t[:, 24, 0:We.shape[0]]
        raw_wq = we_t[:, 18:18 + NODES, :]
        w_time_t = sb("w_time_t", [P, 7, D])
        def halves(t):
            return [t[:, k * BANK:(k + 1) * BANK] for k in range(t.shape[1] // BANK)]

        e_ring_f = e_ring[:, :, :].rearrange("p n s -> p (n s)")
        v_aug_1 = v_aug[:, 1, :, :, :].rearrange("p k h d -> p (k h d)")
        mixing_sets = [halves(mixing[:, :, :].rearrange("p n s -> p (n s)"))[:5], halves(q_aug_f[:, 1, 0:5 * BANK]),
                       halves(e_ring_f[:, 0:5 * BANK]), halves(v_aug_1) + halves(src)[:1],
                       halves(k_aug_f[:, 1, 0:5 * BANK]),
                       halves(q_aug_f[:, 1, 5 * BANK:8 * BANK]) + halves(ctxT)]
        mixing_xTs = [mixing_xT[:, :], rden_bc[:, 0:BANK + 1], e_ring_f[:, 7 * BANK:8 * BANK + 1],
                      raw[:, :, :].rearrange("p u s -> p (u s)")[:, 0:BANK + 1],
                      *(k_aug_f[:, 1, k * BANK + k:(k + 1) * BANK + k + 1] for k in (5, 6))]
        x_nat = [node_ring[:, b, 1, :] for b in range(B)]

        def load_x(b):
            dma(x_nat[b].rearrange("p (k c) -> p k c", c=D), x[b].rearrange("(k p) c -> p k c", p=P), d_x[b])

        load_x(0)
        for i, w in enumerate((Wk, Wv, Wr, Wo)):
            dma(raw_w[:, W_TIME + i, :], w, d_time)
        column(col[:, C_TD:C_TD + 1], time_decay, d_time)
        for i, m in enumerate((mix_k, mix_v, mix_r)):
            column(col[:, C_MIX + i:C_MIX + i + 1], m.rearrange("a b c -> (a b c)"), d_time)
        column(col[:, C_LNG:C_LNG + 1], ln_g, d_time)
        column(col[:, C_LNB:C_LNB + 1], ln_b, d_time)
        time_in = d_time.now()
        load_x(1)
        spread(col[:, C_EW:C_EW + 3 * NODES], ew.rearrange("a b -> (a b)"), 3 * NODES)
        spread(col[:, C_ACTW:C_ACTW + NODES], act_w, NODES)
        dma(be_rows, be, d_weights)
        for c in range(NODES):
            (eq, ek_, ev), _ = node_sources(c)
            dma(w_edge_q[:, c, :], We[eq], d_weights)
            dma(raw_w[:, WE_KV + c, :], We[ek_], d_weights)
            dma(raw_w[:, WE_KV + NODES + c, :], We[ev], d_weights)
        for dst, w in ((raw_w[:, W_KV:W_KV + NODES, :], fWk), (raw_w[:, W_KV + NODES:W_KV + 2 * NODES, :], fWv),
                       (raw_wq, fWq), (w_o[:, :, :], fWo)):
            dma(dst, w.rearrange("n i o -> i n o"), d_weights)
        spread(out_g[:, :], fln_g, D)
        spread(out_b[:, :], fln_b, D)
        weights_in = d_weights.now()
        for b in range(2, B):
            load_x(b)

        neg_half_done = gp(lambda e: e.memset(neg_half[:, :], -0.5), ())
        done = gp(lambda e: e.memset(ident[:, :], 0.0), ())
        ident_done = gp(lambda e: e.affine_select(
            out=ident[:, :], in_=ident[:, :], compare_op=ALU.not_equal, fill=1.0, base=0,
            pattern=[[-1, P]], channel_multiplier=1), [done])
        ones_v_done = [gp(lambda e: e.memset(v_aug[:, 0, :, :, DH:VW], 1.0), ()), None]

        td_done = activate(col[:, C_TD:C_TD + 1], col[:, C_TD:C_TD + 1], ACT.Exp, [time_in])
        omm_done = vec(lambda e: e.tensor_scalar(col[:, C_OMM:C_OMM + 3], col[:, C_MIX:C_MIX + 3], -1.0, 1.0,
                                                 ALU.mult, ALU.add), [time_in])

        banks_used = [0]

        def any_bank():
            banks_used[0] += 1
            return banks_used[0] % PROLOGUE_MISC[0]

        def misc_bank():
            return MISC_BANK

        PROLOGUE_MISC = (4, 5, 6, 7)
        misc_used = [0]

        def bank_of(u):
            if u > 0:
                return MISC_BANK
            misc_used[0] += 1
            return PROLOGUE_MISC[misc_used[0] % len(PROLOGUE_MISC)]

        def fill(i, waits, write, n=1):
            done = None
            for j in range(n):
                done = write(j, bank[i], [*waits, bank_free[i]] if j == 0 else (), pe_misc if j == n - 1 else None)
            return done

        def turn_four(i, srcs, waits):
            return fill(i, waits, lambda j, bk, w, s: transpose(bk[:, j * P:(j + 1) * P], srcs[j], w, s), len(srcs))

        folds = {}

        def time_weights():
            i = any_bank()
            done = turn_four(i, [raw_w[:, W_TIME + j, :] for j in range(4)], [ident_done, time_in])
            for n in range(3):
                for k, cc in enumerate((C_MIX, C_OMM)):
                    activate(w_time_t[:, 2 * n + k, :], bank[i][:, n * P:(n + 1) * P], ACT.Copy, [done, omm_done],
                             scale=col[:, cc + n:cc + n + 1])
            bank_free[i] = folds["time"] = activate(w_time_t[:, 6, :], bank[i][:, 3 * P:4 * P], ACT.Copy, [done])

        def edge_transposes(k):
            def run():
                i = any_bank()
                done = turn_four(i, [raw_w[:, WE_KV + k + j, :] for j in range(4)], [ident_done, weights_in])
                bank_free[i] = folds["edge"] = activate(we_t[:, k:k + 4, :].rearrange("p n d -> p (n d)"), bank[i][:, :],
                                                        ACT.Copy, [done])
            return run

        def bias_columns():
            i = any_bank()
            n = We.shape[0]
            done = fill(i, [ident_done, weights_in], lambda j, bk, w, s: pe.add(lambda e: e.transpose(
                bk[:, 0:n], be_rows, ident[0:n, 0:n]), w, s))
            bank_free[i] = folds["be"] = activate(be_cols, bank[i][:, 0:n], ACT.Copy, [done])

        def reorder_heads():
            for dst, raw_ in ((w_k_fold, raw_w[:, W_KV:W_KV + NODES, :]), (w_q, raw_wq)):
                folds["order"] = vec(lambda e, dst=dst, raw_=raw_: e.tensor_copy(
                    dst[:, :, :].rearrange("p n (d h) -> p n d h", h=H), raw_.rearrange("p n (h d) -> p n d h", h=H)), [weights_in])

        def fold(c):
            (eq, ek_, ev), _ = node_sources(c)
            ewq, ewk, ewv = (col[:, C_EW + 3 * c + i:C_EW + 3 * c + i + 1] for i in range(3))
            wk, wv = w_k_fold[:, c, :], raw_w[:, W_KV + NODES + c, :]
            be_rep = we_t[:, 12 + c, :]

            def products():
                rep = activate(be_rep, be_cols[:, ev:ev + 1].to_broadcast([P, P]), ACT.Copy, [folds["be"]])
                operands = ((we_t[:, c, :], wk), (we_t[:, NODES + c, :], wv), (be_rep, wv),
                            (wk, be_cols[:, ek_:ek_ + 1]))
                i = any_bank()
                done = fill(i, [folds["edge"], folds["be"], rep, folds["order"]], lambda j, bk, w, s: mm(
                    bk[:, j * P:j * P + operands[j][1].shape[-1]], operands[j][0], operands[j][1], w, s), 4)
                for j, (dst, n, s) in enumerate(((w_k_fold[:, c, :], P, ewk), (w_v_fold[:, c, :], P, ewv),
                                                 (v_bias[:, c, :], P, ewv), (col[:, C_BK + c:C_BK + c + 1], 1, ewk))):
                    bank_free[i] = activate(dst, bank[i][:, j * P:j * P + n], ACT.Copy, [done], scale=s)
                for dst, from_, s in ((w_edge_q[:, c, :], w_edge_q[:, c, :], ewq),
                                      (w_o[:, c, :], w_o[:, c, :], col[:, C_ACTW + c:C_ACTW + c + 1]),
                                      (col[:, C_BQ + c:C_BQ + c + 1], be_cols[:, eq:eq + 1], ewq)):
                    folds[c] = activate(dst, from_, ACT.Copy, [weights_in, folds["be"]], scale=s)
            return products

        def weights_of(c):
            return [folds[c], folds["order"]]

        def everything():
            return [s.now() for s in (pe_misc, act_misc, dve_misc)]

        def both(*fs):
            def run():
                for f in fs:
                    if f is not None:
                        f()
            return run

        def norm_stages(dst, src_, eps, area, state, before, free=lambda: [], twice=False):
            s3, d3 = (t.rearrange("p (k c) -> p k c", c=D) for t in (src_, dst))
            of_variance = (1.0 + eps, eps * eps) if twice else (1.0, eps)

            def statistics():
                for k in range(CPB):
                    state["s"] = vec(lambda e, k=k: e.bn_stats(stats[:, area, k, :], s3[:, k, :]), [state[before]])

            def inverse():
                for k in range(CPB):
                    done = vec(lambda e, k=k: e.bn_aggr(meanvar[:, area, k, :], stats[:, area, k, :]), [state["s"]])
                done = vec(lambda e: e.tensor_scalar(vareps[:, area, :], meanvar[:, area, :, 1], *of_variance, ALU.mult, ALU.add), [done])
                state["r"] = gp(lambda e: e.tensor_tensor(rstd[:, area, :], vareps[:, area, :], neg_half[:, :], ALU.pow),
                                      [done, neg_half_done])

            def apply():
                waits = free()
                for k in range(CPB):
                    state["n"] = vec(lambda e, k=k: e.tensor_scalar(
                        d3[:, k, :], s3[:, k, :], meanvar[:, area, k, 0:1], rstd[:, area, k:k + 1], ALU.subtract, ALU.mult),
                        [state["r"], *waits])
            return [statistics, inverse, apply]

        node_ready = [None] * B
        FREE_AFTER = 3 + 1 + 3 + 3
        carried = {}

        def mixing_stages(b, hf, which, take_bank, shared=False):
            y, ek, ekv, er, num = mixing_sets[which]
            xT = mixing_xTs[which]
            xs = x_nat[b][:, hf * BANK:(hf + 1) * BANK]
            cols = slice(hf * BANK, (hf + 1) * BANK)
            td = col[:, C_TD:C_TD + 1].to_broadcast([P, BANK])
            st = {"x": d_x[b].now()}
            area = 2 * b + hf
            free = everything if shared else (lambda: [])
            stages = norm_stages(y, xs, LN_EPS, area, st, "x", free, twice=True)

            def turn():
                st["i"] = i = take_bank()
                st["t"] = turn_four(i, [y[:, j * P:(j + 1) * P] for j in range(CPB)], [st["n"], ident_done])

            def turned():
                i = st["i"]
                if hf == 0:
                    pad = vec(lambda e: e.memset(xT[:, 0:1], 0.0), free())
                else:
                    prev_xT, prev_done = carried[b, "xT"]
                    pad = vec(lambda e: e.tensor_copy(xT[:, 0:1], prev_xT[:, BANK:BANK + 1]), [prev_done, *free()])
                bank_free[i] = st["xT"] = activate(xT[:, 1:BANK + 1], bank[i][:, :], ACT.Identity, [st["t"], pad, *free()],
                                                   bias=col[:, C_LNB:C_LNB + 1], scale=col[:, C_LNG:C_LNG + 1])
                carried[b, "xT"] = (xT, st["xT"])
            stages.append((turn, turned))
            for n in range(3):
                def project(n=n):
                    st["i"] = i = take_bank()
                    st["p"] = fill(i, [st["xT"], folds["time"]], lambda j, bk, w, s: mm(
                        bk[:, :], w_time_t[:, 2 * n + j, :], xT[:, 1 - j:BANK + 1 - j], w, s, start=(j == 0), stop=(j == 1)), 2)

                def projected(n=n):
                    i = st["i"]
                    if n == 0:
                        bank_free[i] = st["k"] = activate(ek, bank[i][:, :], ACT.Exp, [st["p"], *free()])
                    elif n == 1:
                        bank_free[i] = st["v"] = vec(lambda e: e.tensor_tensor(ekv, bank[i][:, :], ek, ALU.mult),
                                                             [st["p"], st["k"], *free()])
                    else:
                        bank_free[i] = st["r0"] = activate(er, bank[i][:, :], ACT.Exp, [st["p"], *free()],
                                                              scale=-1.0)
                stages.append((project, projected))
            den = y

            def scan(dst, data, key):
                def run():
                    start, before = (0.0, None) if hf == 0 else carried[b, key]
                    st[key] = vec(lambda e: e.tensor_tensor_scan(dst, td, data, start, ALU.mult, ALU.add),
                                  [td_done, st["k"], st["v"], before, *free()])
                    keep = carried_col[:, b, ("den", "num").index(key):("den", "num").index(key) + 1]
                    if hf == 0:
                        carried[b, key] = (keep, vec(lambda e: e.tensor_copy(keep, dst[:, BANK - 1:BANK]), [st[key]]))
                return run

            def one_more():
                if shared:
                    st["r1"] = gp(lambda e: e.tensor_scalar(er, er, 1.0, None, ALU.add), [st["r0"]])
                else:
                    st["r1"] = activate(er, er, ACT.Copy, [st["r0"]], bias=1.0)

            def product():
                st["q"] = vec(lambda e: e.scalar_tensor_tensor(out=er, in0=den, scalar=WKV_EPS, in1=er, op0=ALU.add, op1=ALU.mult),
                              [st["den"], st["r1"]])

            def invert(k):
                def run():
                    st["inv"] = vec(lambda e: e.reciprocal(ek[:, k * P:(k + 1) * P], er[:, k * P:(k + 1) * P]), [st["q"], st["den"]])
                return run

            def gate():
                st["g"] = (gp if shared else vec)(lambda e: e.tensor_tensor(ekv, num, ek, ALU.mult), [st["inv"], st["num"]])

            def out_project():
                st["i"] = i = take_bank()
                st["o"] = fill(i, [st["g"]], lambda j, bk, w, s: mm(
                    bk[:, j * P:(j + 1) * P], ekv[:, j * P:(j + 1) * P], w_time_t[:, 6, :], w, s), CPB)

            def residual():
                i = st["i"]
                bank_free[i] = st["x2"] = vec(lambda e: e.tensor_tensor(xs, bank[i][:, :], xs, ALU.add), [st["o"]])

            def store_x2():
                dma(x2_dram[b, :, hf * CPB:(hf + 1) * CPB, :], xs.rearrange("p (k c) -> p k c", c=D), d_x2_out[b], [st["x2"]])

            stages += [both(one_more, scan(den, ek, "den")), scan(num, ekv, "num"), product]
            assert not shared or len(stages) == FREE_AFTER
            stages += [both(invert(k), invert(k + 1)) for k in range(0, CPB, 2)] + [gate, (out_project, residual)]
            last_norm = norm_stages(num, xs, LN_EPS, area, st, "x2", free)
            stages += [both(store_x2, last_norm[0]), *last_norm[1:]]

            def turn_out():
                st["i"] = i = take_bank()
                st["t"] = turn_four(i, [num[:, j * P:(j + 1) * P] for j in range(CPB)], [st["n"]])

            def turned_out():
                i = st["i"]
                bank_free[i] = node_ready[b] = activate(node_ring[:, b, 0, cols], bank[i][:, :], ACT.Copy, [st["t"]])
                carried[b, "end", hf] = node_ready[b]
                if hf == NHALF - 1:
                    dma(node_dram[0, b], node_ring[:, b, 0, :], d_spill[b], [node_ready[b], carried[b, "end", 0]])
            stages.append((turn_out, turned_out))
            return stages

        def run_stage(stage):
            for f in (stage if isinstance(stage, tuple) else (stage,)):
                f()

        def run_side_by_side(lists):
            for t in range(max(o + len(l) for o, l in lists)):
                for o, l in lists:
                    if 0 <= t - o < len(l):
                        run_stage(l[t - o])

        weights_done = []
        ones_k_done = [None, None]

        def end_weights():
            weights_done.extend([pe_misc.now(), act_misc.now(), folds["order"]])

        def ones_k(u, k):
            def run():
                ones_k_done[u] = gp(lambda e: e.memset(
                    k_aug[SPLIT_ROWS:AUG_ROWS, u, 2 * k:2 * k + 2, :].rearrange("p h s -> p (h s)"), 1.0), weights_done)
            return run

        counts = dict(st=0, mx=0)
        e_free = [None] * E_SLOTS
        aug_in, part_out = {}, {}
        max_rows_in = {}
        v_ready, v_read = {}, {}
        ctx_moved = {}
        last_st = {}

        def misc_fill(waits, write, n=1):
            return fill(MISC_BANK, waits, write, n)

        src_read = [None]

        def load_source(u, which):
            c, b = divmod(u, B)
            if c > 0:
                dma(src[:, :], node_dram[node_sources(c)[1][which] + 1, b], d_src, [d_spill[b].now(), src_read[0]])

        def source(u, cols):
            c, b = divmod(u, B)
            return (node_ring[:, b, 0, cols], node_ready[b]) if c == 0 else (src[:, cols], d_src.now())

        def project_q(u, hf):
            c, b = divmod(u, B)
            cols = slice(hf * BANK, (hf + 1) * BANK)
            i = bank_of(u)
            done = fill(i, [node_ready[b], *weights_of(c)], lambda j, bk, w, s: mm(
                bk[:, :], w_edge_q[:, c, :], node_ring[:, b, c % 2, cols], w, s))
            bank_free[i] = activate(node_ring[:, b, (c + 1) % 2, cols], bank[i][:, :], ACT.Identity,
                                    [done, d_spill[b].now(), d_x2_out[b].now()], bias=col[:, C_BQ + c:C_BQ + c + 1])
            return bank_free[i]

        q_done = {}
        split_done = {}
        head_bank = {}

        def project_head(u, side, hf):
            c, b = divmod(u, B)
            cols = slice(hf * BANK, (hf + 1) * BANK)
            w_ = (w_q, w_k_fold)[side][:, c, :]
            data, ready = (node_ring[:, b, (c + 1) % 2, cols], q_done.get((u, hf))) if side == 0 else source(u, cols)
            i = head_bank[u, side, hf] = bank_of(u)
            done = fill(i, [ready, *weights_of(c)], lambda j, bk, w, s: mm(bk[:, :], w_, data, w, s))
            if side == 1:
                src_read[0] = done
            p1 = part[side][:, 0, cols]
            bias = col[:, C_BK + c:C_BK + c + 1]
            if side == 0:
                p1_done = activate(p1, bank[i][:, :], ACT.Copy, [done, d_part[side].now()])
            else:
                p1_done = activate(p1, bank[i][:, :], ACT.Identity, [done, d_part[side].now()], bias=bias)
            split_done[u, side, hf, 1] = p1_done

        def split_rest(u, side, hf):
            c, _ = divmod(u, B)
            cols = slice(hf * BANK, (hf + 1) * BANK)
            p1, r = part[side][:, 0, cols], rest[:, cols]
            bias = 0.0 if side == 0 else col[:, C_BK + c:C_BK + c + 1]
            waits = [split_done[u, side, hf, 1], split_done.get((u, 1) if side == 0 else (u - 1, 0))]
            i = head_bank[u, side, hf]
            if side == 0:
                bank_free[i] = vec(lambda e: e.tensor_tensor(r, bank[i][:, :], p1, ALU.subtract), waits)
            else:
                bank_free[i] = vec(lambda e: e.scalar_tensor_tensor(
                    out=r, in0=bank[i][:, :], scalar=bias, in1=p1, op0=ALU.add, op1=ALU.subtract), waits)
            split_done[u, side, hf, 2] = bank_free[i]

        def split_low(u, side, hf):
            cols = slice(hf * BANK, (hf + 1) * BANK)
            r, p2, p3 = rest[:, cols], part[side][:, 1, cols], part[side][:, 2, cols]
            done = act.add(lambda e: e.activation(p2, r, ACT.Copy), [split_done[u, side, hf, 2]], act_misc)
            split_done[u, side] = gp(lambda e: e.tensor_tensor(p3, r, p2, ALU.subtract), [done])

        def store_parts(u, side):
            part_out[u, side] = dma(part_dram[u % 2, side].rearrange("p r s -> r p s"), part[side][:, :, :], d_part[side],
                                    [split_done[u, side]])

        def load_aug(u, sides=(0, 1)):
            waits = [*(part_out[u, side] for side in sides), last_st.get(u - 2), *weights_done]
            n_sets = H // HG if u < B else 1
            for k in range(n_sets):
                heads = slice(k * H // n_sets, (k + 1) * H // n_sets)
                for side in sides:
                    aug, slots = ((q_aug, Q_SLOTS), (k_aug, K_SLOTS))[side]
                    for slot, p, n in ascending_runs(slots):
                        done = dma(aug[slot * DH:(slot + n) * DH, u % 2, heads, :],
                                   part_dram[u % 2, side, p:p + n].rearrange("p (d h) s -> (p d) h s", h=H)[:, heads, :],
                                   d_aug[k], waits)
                for hg in range(k * H // HG // n_sets, (k + 1) * H // HG // n_sets):
                    aug_in[u, hg] = done

        def project_v(u, hf):
            c, _ = divmod(u, B)
            k0 = hf * CPB
            data, ready = source(u, slice(k0 * P, (k0 + CPB) * P))
            i = bank_of(u)
            done = src_read[0] = fill(i, [ready, *weights_of(c)], lambda j, bk, w, s: mm(
                bk[:, j * P:(j + 1) * P], data[:, j * P:(j + 1) * P], w_v_fold[:, c, :], w, s), CPB)
            bias = v_bias[:, c, :].rearrange("p (o h d) -> p o h d", o=1, h=H).to_broadcast([P, CPB, H, DH])
            bank_free[i] = v_ready[u] = vec(lambda e: e.tensor_tensor(
                v_aug[:, u % 2, k0:k0 + CPB, :, 0:DH],
                bank[i][:, :].rearrange("p (k h d) -> p k h d", k=CPB, h=H), bias, ALU.add),
                [done, v_read.get(u - 2), ones_v_done[u % 2]])

        def max_rows(G):
            u, g = divmod(G, GPU)
            hg, qh = divmod(g, NHALF)
            r = G % 2
            NR = HG * CPB
            state = {}

            def combine():
                state["col"] = combined[G] = vec(lambda e: e.tensor_reduce(max_col[:, r, :], max_half[:, r, :, :], AX_X, ALU.max),
                                                 [dve_max.now()])

            def turn():
                i = state["i"] = MAX_BANKS[counts["mx"] % len(MAX_BANKS)]
                counts["mx"] += 1
                state["t"] = pe.add(lambda e: e.transpose(bank[i][0:NR, 0:P], max_col[:, r, :], ident[:, :]),
                                    [state["col"], bank_free[i]], pe_max)

            def negate():
                i = state["i"]
                state["m"] = bank_free[i] = vec(lambda e: e.tensor_scalar(
                    max_neg[:, r, :], bank[i][0:NR, 0:P], -1.0, None, ALU.mult), [state["t"], splits.get(G - 2)])

            p = [max_part[:, r, i, :] for i in range(3)]
            neg, left = max_neg[:, r, :], max_rest[:, r, :]

            def split():
                gp(lambda e: e.tensor_copy(p[0], neg), [state["m"], d_max_out[r].now()])
                gp(lambda e: e.tensor_tensor(left, neg, p[0], ALU.subtract), [])
                gp(lambda e: e.tensor_copy(p[1], left), [])
                splits[G] = state["s"] = gp(lambda e: e.tensor_tensor(p[2], left, p[1], ALU.subtract), [])

            def move():
                o = dma(max_dram[r].rearrange("i n s -> n i s"), max_part[:, r, :, :], d_max_out[r], [state["s"]])
                max_rows_in[G] = dma(
                    q_aug[SPLIT_ROWS:AUG_ROWS, u % 2, hg * HG:(hg + 1) * HG, qh * BANK:(qh + 1) * BANK],
                    max_dram[r].rearrange("i (h t) s -> i h (t s)", h=HG), d_max_in[r], [o, last_st.get(u - 2)])
            combine()
            return {0: [None, both(turn, negate)], 1: [split, None], 2: [move, None]}

        splits = {}

        def evacuate_ctx(G, pv_done):
            u, g = divmod(G, GPU)
            hg, qh = divmod(g, NHALF)
            r = G % 2
            bank_free[CTX_BANK] = done = activate(raw[:, r, :], bank[CTX_BANK][:, :], ACT.Copy,
                                                  [pv_done, d_ctx[r].now(), d_last_den.now()])

            def move():
                cols = slice(qh * BANK, (qh + 1) * BANK)
                if u == UNITS - 1:
                    for j in range(HG):
                        h = hg * HG + j
                        last_den_in[qh] = dma(last_den[h * DH:(h + 1) * DH, cols], raw[j * VW + DH:(j + 1) * VW, r, :],
                                              d_last_den, [done])
                for j in range(HG):
                    h = hg * HG + j
                    dma(ctxT[h * DH:(h + 1) * DH, cols], raw[j * VW:j * VW + DH, r, :], d_ctx[r], [done, out_read.get(u - 1)])
                    ctx_moved[G] = d_ctx[r].now()
                if u < UNITS - 1:
                    ctx_moved[G] = dma(den_dram[u % 2, hg * HG:(hg + 1) * HG, cols], raw[DH:P:VW, r, :], d_ctx[r], [done])
            return move

        out_read = {}

        def finish_unit(u):
            c, b = divmod(u, B)
            state = {}

            def load_den():
                dma(den_pack[:, :], den_dram[u % 2].rearrange("h (a s) -> (h a) s", s=H * S // P), d_den_in,
                    [ctx_moved[u * GPU + g] for g in range(GPU)])

            def reciprocal():
                state["r"] = vec(lambda e: e.reciprocal(rden_pack[:, :], den_pack[:, :]), [d_den_in.now(), d_rden_out.now()])

            def spread_rden():
                o = dma(rden_dram[u % 2].rearrange("h (a s) -> (h a) s", s=H * S // P), rden_pack[:, :], d_rden_out, [state["r"]])
                for h in range(H):
                    dma(rden_bc[h * DH:(h + 1) * DH, :], rden_dram[u % 2, h:h + 1, :].to_broadcast([DH, S]), d_rden_in,
                        [o, pool_misc.now(), dve_misc.now()])

            def normalise():
                state["n"] = gp(lambda e: e.tensor_tensor(ctxT[:, :], ctxT[:, :], rden_bc[:, :], ALU.mult),
                                      [d_rden_in.now(), ctx_moved[u * GPU + GPU - 1], ctx_moved[u * GPU + GPU - 2]])

            def project(hf):
                def run():
                    cols = slice(hf * BANK, (hf + 1) * BANK)
                    node = node_ring[:, b, (c + 1) % 2, cols]
                    done = misc_fill([state["n"]], lambda j, bk, w, s: mm(bk[:, :], w_o[:, c, :], ctxT[:, cols], w, s))
                    bank_free[MISC_BANK] = node_ready[b] = vec(lambda e: e.tensor_tensor(node, bank[MISC_BANK][:, :], node, ALU.add), [done])
                    out_read[u] = done
                return run

            def spill():
                if c < SPILLED:
                    dma(node_dram[c + 1, b], node_ring[:, b, (c + 1) % 2, :], d_spill[b], [node_ready[b]])
            stages = {3: [load_den], 5: [reciprocal], 6: [spread_rden], 11: [normalise], 13: [project(0)], 14: [project(1)]}
            stages.update(finish_batch(u) if c == NODES - 1 else {15: [spill]})
            return stages

        def finish_batch(u):
            c, b = divmod(u, B)
            y, x2 = rden_bc, src
            yb = y[:, :]
            state = {}

            def turn(hf):
                def run():
                    k0 = hf * CPB
                    done = misc_fill([node_ready[b]], lambda j, bk, w, s: transpose(
                        bk[:, j * P:(j + 1) * P], node_ring[:, b, (c + 1) % 2, (k0 + j) * P:(k0 + j + 1) * P], w, s), CPB)
                    bank_free[MISC_BANK] = state["y"] = activate(y[:, k0 * P:(k0 + CPB) * P], bank[MISC_BANK][:, :], ACT.Copy, [done])
                    if hf == 0:
                        dma(x2[:, :].rearrange("p (k c) -> p k c", c=D), x2_dram[b], d_x2_in, [src_read[0], d_x2_out[b].now()])
                return run

            halves = [norm_stages(yb[:, hf * BANK:(hf + 1) * BANK], yb[:, hf * BANK:(hf + 1) * BANK], LN_EPS_OUT, 2 * B, state, "y")
                      for hf in range(NHALF)]

            def affine():
                y3 = yb.rearrange("p (k c) -> p k c", c=D)
                g3, b3 = (t[:, :].rearrange("p (o c) -> p o c", o=1).to_broadcast([P, NCH, D]) for t in (out_g, out_b))
                a = gp(lambda e: e.tensor_tensor(y3, y3, g3, ALU.mult), [state["n"]])
                a = gp(lambda e: e.tensor_tensor(y3, y3, b3, ALU.add), [a])
                state["o"] = src_read[0] = gp(lambda e: e.tensor_tensor(yb, yb, x2[:, :], ALU.add), [a, d_x2_in.now()])

            def store():
                dma(out[b].rearrange("(k p) c -> p k c", p=P), yb.rearrange("p (k c) -> p k c", c=D), d_out, [state["o"]])
            return {15: [turn(0)], 16: [turn(1)], 17: halves[0][:2], 18: [halves[0][2], halves[1][0]], 19: halves[1][1:],
                    20: [affine], 22: [store]}

        last_den, last_y, last_x2 = (mixing[:, :, :].rearrange("p n s -> p (n s)")[:, k * S:(k + 1) * S] for k in range(3))
        last_den_in = {}

        def finish_last(hf):
            u = UNITS - 1
            c, b = divmod(u, B)
            k0 = hf * CPB
            cols = slice(hf * BANK, (hf + 1) * BANK)
            node, y, x2, den = node_ring[:, b, (c + 1) % 2, cols], last_y[:, cols], last_x2[:, cols], last_den[:, cols]
            y3, x3 = (t.rearrange("p (k c) -> p k c", c=D) for t in (y, x2))
            state = {}

            def load_x2():
                state["x2"] = dma(x3, x2_dram[b][:, k0:k0 + CPB, :], d_x2_last[hf], [d_x2_out[b].now()])

            def invert(k):
                def run():
                    state["r"] = vec(lambda e: e.reciprocal(den[:, k * P:(k + 1) * P], den[:, k * P:(k + 1) * P]), [last_den_in[hf]])
                return run

            def normalise():
                state["c"] = vec(lambda e: e.tensor_tensor(ctxT[:, cols], ctxT[:, cols], den, ALU.mult),
                                 [state["r"], *(ctx_moved[u * GPU + g * NHALF + hf] for g in range(H // HG))])

            def project():
                done = misc_fill([state["c"]], lambda j, bk, w, s: mm(bk[:, :], w_o[:, c, :], ctxT[:, cols], w, s))
                bank_free[MISC_BANK] = state["o"] = vec(lambda e: e.tensor_tensor(node, bank[MISC_BANK][:, :], node, ALU.add), [done])

            def turn():
                done = misc_fill([state["o"]], lambda j, bk, w, s: transpose(
                    bk[:, j * P:(j + 1) * P], node[:, j * P:(j + 1) * P], w, s), CPB)
                bank_free[MISC_BANK] = state["y"] = activate(y, bank[MISC_BANK][:, :], ACT.Copy, [done])

            def affine():
                g3, b3 = (t[:, :].rearrange("p (o c) -> p o c", o=1).to_broadcast([P, CPB, D]) for t in (out_g, out_b))
                vec(lambda e: e.tensor_tensor(y3, y3, g3, ALU.mult), [state["n"]])
                vec(lambda e: e.tensor_tensor(y3, y3, b3, ALU.add), [dve_misc.now()])
                state["z"] = vec(lambda e: e.tensor_tensor(y, y, x2, ALU.add), [dve_misc.now(), state["x2"]])

            def store():
                dma(out[b, k0 * P:(k0 + CPB) * P, :].rearrange("(k p) c -> p k c", p=P), y3, d_out, [state["z"]])
            return [load_x2, *(invert(k) for k in range(CPB)), normalise, project, turn,
                    *norm_stages(y, y, LN_EPS_OUT, 2 * B, state, "y"), affine, store]

        def q_of(u, hf):
            def run():
                q_done[u, hf] = project_q(u, hf)
            return run

        def projection_stages(u):
            return {0: [q_of(u, 0)], 1: [q_of(u, 1)],
                    2: [lambda: project_head(u, 1, 0), lambda: split_rest(u, 1, 0)],
                    3: [lambda: project_head(u, 1, 1), lambda: split_rest(u, 1, 1)],
                    4: [lambda: split_low(u, 1, 0), lambda: split_low(u, 1, 1)],
                    5: [lambda: project_head(u, 0, 0), lambda: split_rest(u, 0, 0)],
                    6: [lambda: (store_parts(u, 1), project_head(u, 0, 1)), lambda: split_rest(u, 0, 1)],
                    7: [lambda: split_low(u, 0, 0), lambda: split_low(u, 0, 1)],
                    8: [lambda: store_parts(u, 0)], 9: [lambda: load_aug(u)]}

        def score_tile(G, chunk, j):
            u, g = divmod(G, GPU)
            hg, qh = divmod(g, NHALF)
            h = hg * HG + j
            n = counts["st"]
            counts["st"] += 1
            i = ST_BANKS[n % len(ST_BANKS)]
            last_st[u] = done = mm(bank[i][:, :], k_aug[0:AUG_ROWS, u % 2, h, chunk * P:(chunk + 1) * P],
                                   q_aug[0:AUG_ROWS, u % 2, h, qh * BANK:(qh + 1) * BANK],
                                   [bank_free[i], max_rows_in[G], aug_in[u, hg], ones_k_done[u % 2]], pe_st)
            bank_free[i] = act.add(lambda e: e.activation(e_ring[:, n % E_SLOTS, :], bank[i][:, :], ACT.Exp, scale=EXP_SCALE),
                                 [done, e_free[n % E_SLOTS]], act_exp)
            return n % E_SLOTS, bank_free[i]

        def max_tile(G, t):
            u, g = divmod(G, GPU)
            hg, qh = divmod(g, NHALF)
            row, kh = divmod(t, NHALF)
            j, qt = divmod(row, CPB)
            h = hg * HG + j
            q0 = qh * BANK + qt * P
            i = MAX_BANKS[counts["mx"] % len(MAX_BANKS)]
            counts["mx"] += 1
            done = mm(bank[i][:, :], q_aug[0:SPLIT_ROWS, u % 2, h, q0:q0 + P],
                      k_aug[0:SPLIT_ROWS, u % 2, h, kh * BANK:(kh + 1) * BANK], [bank_free[i], aug_in[u, hg]], pe_max)
            bank_free[i] = dve.add(lambda e: e.tensor_reduce(max_half[:, G % 2, row, kh:kh + 1], bank[i][:, :],
                                                            AX_X, ALU.max), [done, combined.get(G - 2)], dve_max)

        combined = {}

        def context(G, chunk, tiles):
            u, g = divmod(G, GPU)
            hg = g // NHALF
            for j, (slot, ready) in enumerate(tiles):
                done = mm(bank[CTX_BANK][j * VW:(j + 1) * VW, :], v_aug[:, u % 2, chunk, hg * HG + j, :], e_ring[:, slot, :],
                          [ready, v_ready[u], bank_free[CTX_BANK] if chunk == 0 else None], pe_ctx if j == HG - 1 else None,
                          start=(chunk == 0), stop=(chunk == NCH - 1))
            for slot, _ in tiles:
                e_free[slot] = done
            v_read[u] = done
            return done

        due = {}

        def schedule(at, stages):
            for chunk, halves in stages.items():
                for k, stage in enumerate(halves):
                    if stage is None:
                        continue
                    due.setdefault(2 * (at + chunk) + k, []).append(stage)

        UNIT_CHUNKS = GPU * NCH
        MAX_TILES = HG * CPB * NHALF // NCH

        taken = set()

        def reserve(at, stages, fills):
            schedule(at, stages)
            assert not taken & {at + k for k in fills}
            taken.update(at + k for k in fills)

        def place(at, stages, pace=1):
            half = 2 * at
            for stage in stages:
                if isinstance(stage, tuple):
                    half += half % 2
                    while half // 2 in taken:
                        half += 2
                    taken.add(half // 2)
                    schedule(half // 2, {0: list(stage)})
                    half += 2
                else:
                    due.setdefault(half, []).append(stage)
                    half += pace
            return -(-half // 2)

        PROJECT_AT = [None, 1] + [0] * (UNITS - 2)
        VALUES_AT, LOAD_VALUES_AT = (26, 27), 23
        for u in range(UNITS):
            if u > 0:
                slot = (u - 1) * UNIT_CHUNKS
                at = PROJECT_AT[u]
                schedule(slot, {0: [lambda u=u: load_source(u, 0)], LOAD_VALUES_AT: [lambda u=u: load_source(u, 1)]})
                reserve(slot, {k: [lambda u=u, hf=hf: project_v(u, hf)] for hf, k in enumerate(VALUES_AT)}, VALUES_AT)
                reserve(slot + at, projection_stages(u), (0, 1, 2, 3, 5, 6))
            if u < UNITS - 1:
                reserve((u + 1) * UNIT_CHUNKS, finish_unit(u), (13, 14) + ((15, 16) if u // B == NODES - 1 else ()))
        load_x2, *stages = finish_last(0)
        schedule(UNITS * UNIT_CHUNKS - 4, {0: [load_x2, stages[0]], 1: stages[1:3], 2: [stages[3], stages[4]], 3: [stages[5], None],
                                      4: stages[6:8], 5: stages[8:10], 6: stages[10:]})
        load_x2, *stages = finish_last(1)
        schedule(UNITS * UNIT_CHUNKS, {0: [None, load_x2], 3: stages[0:2], 4: stages[2:4], 5: stages[4:6], 6: stages[6:8],
                                       7: stages[8:10], 8: stages[10:]})

        first, second, third = ([mixing_stages(b, hf, 2 * b + hf, any_bank) for hf in range(NHALF)] for b in range(3))
        weight_stages = [edge_transposes(k) for k in range(0, 2 * NODES, 4)] + [bias_columns, reorder_heads]
        weight_stages += [fold(0)]
        fold_stages = [fold(c) for c in range(1, NODES)] + [end_weights]
        UNIT0 = SECOND_HALF + len(first[0])
        unit0 = [
            [lambda: project_head(0, 1, 0), lambda: project_head(0, 1, 1), q_of(0, 0), q_of(0, 1)],
            [lambda: split_rest(0, 1, 0), lambda: split_rest(0, 1, 1)],
            [lambda: project_head(0, 0, 0), lambda: project_head(0, 0, 1), lambda: split_low(0, 1, 0), lambda: split_low(0, 1, 1),
             lambda: store_parts(0, 1)],
            [lambda: load_aug(0, (1,)), lambda: split_rest(0, 0, 0), lambda: split_rest(0, 0, 1)],
            [lambda: split_low(0, 0, 0), lambda: split_low(0, 0, 1), lambda: store_parts(0, 0), lambda: load_aug(0, (0,))],
            [lambda: project_v(0, 0)], [lambda: project_v(0, 1)]]
        unit0 = [both(*fs) for fs in unit0]
        run_side_by_side([(0, [time_weights]), (0, first[0]), (SECOND_HALF, first[1]), (WEIGHTS, weight_stages), (UNIT0, unit0),
                          (UNIT0 + 3 - len(fold_stages), fold_stages),
                          (SECOND_BATCH, second[0]), (SECOND_BATCH + SECOND_HALF, second[1]),
                          (THIRD_BATCH, third[0]), (THIRD_BATCH + SECOND_HALF, third[1])])
        ones_v_done[1] = gp(lambda e: e.memset(v_aug[:, 1, :, :, DH:VW], 1.0), everything())
        start = -LOOKAHEAD
        for k in range(H // 2):
            schedule(start + 2, {2 * k: [ones_k(0, k)]})
            schedule(0, {1 + 2 * k: [ones_k(1, k)]})
        at = 2
        for hf in range(NHALF):
            half = mixing_stages(B - 1, hf, 0, misc_bank, shared=True)
            middle = place(at, half[:FREE_AFTER], pace=2)
            end = place(middle, half[FREE_AFTER:], pace=2)
            at = middle + 1
        assert end <= (B - 2) * UNIT_CHUNKS + PROJECT_AT[B - 1]

        previous = None
        last_step = UNITS * UNIT_CHUNKS + 2 * NCH
        for step in range(-LOOKAHEAD, last_step):
            G, chunk = divmod(step, NCH)
            ahead_G, ahead_chunk = divmod(step + LOOKAHEAD, NCH)
            tiles = []
            for j in range(HG):
                if 0 <= G < GROUPS:
                    tiles.append(score_tile(G, chunk, j))
                if ahead_G < GROUPS:
                    max_tile(ahead_G, ahead_chunk * MAX_TILES + j)
                if j % 2:
                    for stage in due.pop(2 * step + j // 2, ()):
                        stage()
            if previous is not None:
                done = context(*previous)
                if previous[1] == NCH - 1:
                    wait = 6 if previous[0] % GPU == 0 else 0
                    schedule(step + 1, {wait: [evacuate_ctx(previous[0], done)]})
            previous = (G, chunk, tiles) if tiles else None
            if ahead_chunk == NCH - 1 and ahead_G < GROUPS:
                schedule(step + 1, max_rows(ahead_G))
        assert not due, sorted(due)

        sp.add(None, [s.now() for s in signals if s.count])

        with nc.Block() as block:
            @block.tensor
            def _(e):
                pe.play(e)

            @block.scalar
            def _(e):
                act.play(e)

            @block.vector
            def _(e):
                dve.play(e)

            @block.gpsimd
            def _(e):
                pool.play(e)

            @block.sync
            def _(e):
                sp.play(e)


_INS = ["L0_attn_x", "L0_attn_time_decay", "L0_attn_time_mix_k", "L0_attn_time_mix_v", "L0_attn_time_mix_r",
        "L0_attn_Wk", "L0_attn_Wv", "L0_attn_Wr", "L0_attn_Wo", "L0_attn_ln_g", "L0_attn_ln_b", "L0_ffn_ew",
        "L0_ffn_act_w", "L0_ffn_We", "L0_ffn_be", "L0_ffn_Wq", "L0_ffn_Wk", "L0_ffn_Wv", "L0_ffn_Wo",
        "L0_ffn_ln_g", "L0_ffn_ln_b"]


def kernel(**inputs):
    import numpy as _np
    import concourse.bacc as _bacc
    from concourse import mybir as _mybir
    from concourse.bass_utils import run_bass_kernel_spmd as _run

    nc = _bacc.Bacc("TRN2", target_bir_lowering=False, num_devices=1)
    arrays, args = {}, []
    for name in _INS:
        a = _np.ascontiguousarray(inputs[name])
        arrays[f"in_{name}"] = a
        args.append(nc.dram_tensor(f"in_{name}", a.shape, _mybir.dt.from_np(a.dtype), kind="ExternalInput").ap())
    out = nc.dram_tensor("out_0", arrays["in_L0_attn_x"].shape, F32, kind="ExternalOutput").ap()
    build(nc, *args, out)
    r = _run(nc, [arrays], core_ids=[0])
    return r.results[0]["out_0"]
```
